# Optimizing a Trainium2 kernel written in Bass

```python
import numpy as np
import jax
import jax.numpy as jnp

def _softmax(x, axis=-1):
    return jax.nn.softmax(x, axis=axis)

def _gelu(x):
    return jax.nn.gelu(x, approximate=True)

def _silu(x):
    return jax.nn.silu(x)

def _sigmoid(x):
    return jax.nn.sigmoid(x)

def _layernorm(x, axis=-1, eps=1e-05):
    m = jnp.mean(x, axis=axis, keepdims=True)
    v = jnp.var(x, axis=axis, keepdims=True)
    return (x - m) / jnp.sqrt(v + eps)

def _scatter_add(tgt, idx, src, axis=0):
    return tgt.at[idx].add(src)

def _segment_sum(src, seg, n):
    return jax.ops.segment_sum(src, seg, n)
kernel_name = 'mk_seq_postln_d1_jaxref_r4_46268c'

def setup_inputs(seed: int=0):
    np.random.seed(seed)
    _w = jnp.asarray

    def _L0_attn_setup():
        import jax, jax.numpy as jnp
        import numpy as np
        N_HEADS = 16

        def _alibi_causal_mask(T, n_heads, dtype):
            slopes = (1.0 / jnp.power(2.0, jnp.arange(1, n_heads + 1, dtype=dtype)))[:, None, None]
            idx = jnp.arange(T)
            rel = (idx[None, :] - idx[:, None]).astype(dtype)
            alibi = jnp.tril(rel)
            causal = jnp.where(idx[None, :] > idx[:, None], -jnp.inf, 0.0).astype(dtype)
            return (alibi + causal)[None, :, :] * slopes
        key = jax.random.key(seed)
        ks = jax.random.split(key, 5)
        B, T, C = (2, 512, 256)
        scale = 0.02
        return {'x': jax.random.normal(ks[0], (B, T, C), dtype=jnp.float32), 'W_attn': jax.random.normal(ks[1], (C, 3 * C), dtype=jnp.float32) * scale, 'b_attn': jax.random.normal(ks[2], (3 * C,), dtype=jnp.float32) * scale, 'W_proj': jax.random.normal(ks[3], (C, C), dtype=jnp.float32) * scale, 'b_proj': jax.random.normal(ks[4], (C,), dtype=jnp.float32) * scale}
    _L0_attn_in = _L0_attn_setup()

    def _L0_ffn_setup():
        import jax, jax.numpy as jnp
        import numpy as np
        D_IN, D_HID = (256, 1024)

        def _ternary(key, shape):
            return jax.random.randint(key, shape, -1, 2).astype(jnp.float32)

        def _tlin(x, w, s):
            return jnp.einsum('bsi,oi->bso', x, w) * s
        key = jax.random.key(seed)
        ks = jax.random.split(key, 12)
        inv = lambda fan: 1.0 / np.sqrt(fan).astype(np.float32)
        return {'x': jax.random.normal(ks[0], (4, 512, D_IN), dtype=jnp.float32), 'w1_w': _ternary(ks[1], (D_HID, D_IN)), 'w1_s': jax.random.uniform(ks[2], (D_HID,), dtype=jnp.float32) * inv(D_IN), 'w2_w': _ternary(ks[3], (D_HID, D_IN)), 'w2_s': jax.random.uniform(ks[4], (D_HID,), dtype=jnp.float32) * inv(D_IN), 'h1_w': _ternary(ks[5], (D_HID, D_HID)), 'h1_s': jax.random.uniform(ks[6], (D_HID,), dtype=jnp.float32) * inv(D_HID), 'h2_w': _ternary(ks[7], (D_HID, D_HID)), 'h2_s': jax.random.uniform(ks[8], (D_HID,), dtype=jnp.float32) * inv(D_HID), 'w3_w': _ternary(ks[9], (D_IN, D_HID)), 'w3_s': jax.random.uniform(ks[10], (D_IN,), dtype=jnp.float32) * inv(D_HID)}
    _L0_ffn_in = _L0_ffn_setup()
    _d = {'L0_attn_x': _L0_attn_in['x'], 'L0_attn_W_attn': _L0_attn_in['W_attn'], 'L0_attn_b_attn': _L0_attn_in['b_attn'], 'L0_attn_W_proj': _L0_attn_in['W_proj'], 'L0_attn_b_proj': _L0_attn_in['b_proj'], 'L0_ffn_w1_w': _L0_ffn_in['w1_w'], 'L0_ffn_w1_s': _L0_ffn_in['w1_s'], 'L0_ffn_w2_w': _L0_ffn_in['w2_w'], 'L0_ffn_w2_s': _L0_ffn_in['w2_s'], 'L0_ffn_h1_w': _L0_ffn_in['h1_w'], 'L0_ffn_h1_s': _L0_ffn_in['h1_s'], 'L0_ffn_h2_w': _L0_ffn_in['h2_w'], 'L0_ffn_h2_s': _L0_ffn_in['h2_s'], 'L0_ffn_w3_w': _L0_ffn_in['w3_w'], 'L0_ffn_w3_s': _L0_ffn_in['w3_s']}
    _x0 = _d['L0_attn_x']
    _d['L0_attn_x'] = jax.random.normal(jax.random.fold_in(jax.random.key(seed), 1), (1, 4096, 256), dtype=_x0.dtype)
    del _x0
    return _d

def reference(L0_attn_x, L0_attn_W_attn, L0_attn_b_attn, L0_attn_W_proj, L0_attn_b_proj, L0_ffn_w1_w, L0_ffn_w1_s, L0_ffn_w2_w, L0_ffn_w2_s, L0_ffn_h1_w, L0_ffn_h1_s, L0_ffn_h2_w, L0_ffn_h2_s, L0_ffn_w3_w, L0_ffn_w3_s):

    def _L0_attn_ref(x, W_attn, b_attn, W_proj, b_proj):
        import jax, jax.numpy as jnp
        import numpy as np
        N_HEADS = 16

        def _alibi_causal_mask(T, n_heads, dtype):
            slopes = (1.0 / jnp.power(2.0, jnp.arange(1, n_heads + 1, dtype=dtype)))[:, None, None]
            idx = jnp.arange(T)
            rel = (idx[None, :] - idx[:, None]).astype(dtype)
            alibi = jnp.tril(rel)
            causal = jnp.where(idx[None, :] > idx[:, None], -jnp.inf, 0.0).astype(dtype)
            return (alibi + causal)[None, :, :] * slopes
        B, T, C = x.shape
        H = N_HEADS
        D = C // H
        qkv = x @ W_attn + b_attn
        q, k, v = jnp.split(qkv, 3, axis=-1)
        q = q.reshape(B, T, H, D).transpose(0, 2, 1, 3)
        k = k.reshape(B, T, H, D).transpose(0, 2, 1, 3)
        v = v.reshape(B, T, H, D).transpose(0, 2, 1, 3)
        att = jnp.einsum('bhtd,bhsd->bhts', q, k) / jnp.sqrt(jnp.asarray(D, x.dtype))
        att = att + _alibi_causal_mask(T, H, x.dtype)[None]
        att = jax.nn.softmax(att, axis=-1)
        y = jnp.einsum('bhts,bhsd->bhtd', att, v)
        y = y.transpose(0, 2, 1, 3).reshape(B, T, C)
        return y @ W_proj + b_proj

    def _L0_ffn_ref(x, w1_w, w1_s, w2_w, w2_s, h1_w, h1_s, h2_w, h2_s, w3_w, w3_s):
        import jax, jax.numpy as jnp
        import numpy as np
        D_IN, D_HID = (256, 1024)

        def _ternary(key, shape):
            return jax.random.randint(key, shape, -1, 2).astype(jnp.float32)

        def _tlin(x, w, s):
            return jnp.einsum('bsi,oi->bso', x, w) * s
        h = jax.nn.silu(_tlin(x, w1_w, w1_s)) * _tlin(x, w2_w, w2_s)
        h = jax.nn.gelu(_tlin(h, h1_w, h1_s), approximate=False)
        h = jax.nn.gelu(_tlin(h, h2_w, h2_s), approximate=False)
        return _tlin(h, w3_w, w3_s)
    x = L0_attn_x
    x = _layernorm(x + _L0_attn_ref(x, L0_attn_W_attn, L0_attn_b_attn, L0_attn_W_proj, L0_attn_b_proj), axis=-1)
    x = _layernorm(x + _L0_ffn_ref(x, L0_ffn_w1_w, L0_ffn_w1_s, L0_ffn_w2_w, L0_ffn_w2_s, L0_ffn_h1_w, L0_ffn_h1_s, L0_ffn_h2_w, L0_ffn_h2_s, L0_ffn_w3_w, L0_ffn_w3_s), axis=-1)
    return x

_drawn_inputs = setup_inputs


def setup_inputs(seed=0):
    import zlib

    import numpy as np

    out = dict(_drawn_inputs(seed))
    spreads = {}
    factors = {'L0_attn_W_attn': 3.072,
     'L0_attn_b_attn': 7.598,
     'L0_attn_W_proj': 2.872,
     'L0_attn_b_proj': 2.899,
     'L0_ffn_w1_w': 8.0,
     'L0_ffn_w1_s': 8.0,
     'L0_ffn_w2_w': 8.0,
     'L0_ffn_w2_s': 8.0,
     'L0_ffn_h1_w': 8.0,
     'L0_ffn_h1_s': 8.0,
     'L0_ffn_h2_w': 8.0,
     'L0_ffn_h2_s': 8.0,
     'L0_ffn_w3_w': 8.0,
     'L0_ffn_w3_s': 8.0}
    for name, (base, spread) in spreads.items():
        noise = np.random.default_rng([zlib.crc32(name.encode()), seed]).standard_normal(out[name].shape)
        drawn = base * np.exp(spread * noise) if base else spread * noise
        out[name] = jnp.asarray(drawn.astype(out[name].dtype))
    for name, factor in factors.items():
        out[name] = (out[name] * factor).astype(out[name].dtype)
    return out
```

```python
from contextlib import ExitStack

import concourse.bass as bass
from concourse import mybir

ALU = mybir.AluOpType
ACT = mybir.ActivationFunctionType
F32 = mybir.dt.float32
BF16 = mybir.dt.bfloat16
U16 = mybir.dt.uint16
AX_X = mybir.AxisListType.X

P = 128
TB = 512
DMA = 16
EPS = 1e-5

Q_PART = (0, 0, 1, 0, 2, 1)
K_PART = (0, 1, 0, 2, 0, 1)
ALIBI = 4


def project(nc, dram, T, C, H):
    NT = T // TB
    KC = C // P
    MQK = 2 * C // P
    SUB = TB // P
    D = C // H
    G = H // 4
    SCALE = float(D) ** -0.5
    assert NT % 2 == 0 and 2 * D == 32

    with ExitStack() as ctx:
        def sb(name, shape, dt):
            return ctx.enter_context(nc.sbuf_tensor(name, shape, dt))

        def sem(name):
            return ctx.enter_context(nc.semaphore(name))

        xT = sb("xT", [P, 2, KC, TB], F32)
        w_qkv = sb("w_qkv", [P, KC, 3 * C], F32)
        b_qk = sb("b_qk", [P, MQK], F32)
        b_qk_scaled = sb("b_qk_scaled", [P, MQK], F32)
        b_v = sb("b_v", [P, C], F32)
        full = sb("full", [P, 2, TB], F32)
        rest = sb("rest", [P, 2, TB], F32)
        parts = sb("parts", [P, 4, 3, TB], BF16)
        v_ones = sb("v_ones", [P, 2, SUB, G, 4, 2, D], F32)
        qk_psum = ctx.enter_context(nc.psum_tensor("qk_psum", [P, MQK, TB], F32))
        v_psum = ctx.enter_context(nc.psum_tensor("v_psum", [P, SUB // 2, 2, C], F32))

        w_loaded = sem("w_loaded")
        x_loaded = [sem("x_loaded_0"), sem("x_loaded_1")]
        bias_ready = sem("bias_ready")
        ones_ready = sem("ones_ready")
        qk_ready = sem("qk_ready")
        v_ready = sem("v_ready")
        full_ready = sem("full_ready")
        step_done = sem("step_done")
        parts_ready = sem("parts_ready")
        parts_stored = [sem(f"parts_stored_{i}") for i in range(4)]
        v_sb_ready = sem("v_sb_ready")
        v_stored = [sem("v_stored_0"), sem("v_stored_1")]
        waits_passed = sem("waits_passed")
        block = ctx.enter_context(nc.Block())

        @block.sync
        def _(sp):
            sp.dma_start(w_qkv[:], dram["w_attn"].rearrange("(k p) n -> p k n", p=P)).then_inc(w_loaded, DMA)
            sp.dma_start(b_qk[:], dram["b_qk"]).then_inc(w_loaded, DMA)
            sp.dma_start(b_v[:], dram["b_v"]).then_inc(w_loaded, DMA)
            x_src = dram["xT"].rearrange("(k p) (n t) -> n p k t", p=P, t=TB)
            with sp.Fori(0, NT // 2) as i:
                for u in range(2):
                    sp.wait_ge(v_ready, 2 * i + u + 1)
                    sp.dma_start(xT[:, u], x_src[2 * i + u]).then_inc(x_loaded[u], DMA)

        @block.tensor
        def _(pe):
            pe.sem_inc(v_ready, 2)
            pe.wait_ge(w_loaded, 3 * DMA)
            with pe.Fori(0, NT // 2) as i:
                for u in range(2):
                    pe.wait_ge(x_loaded[u], DMA * i + DMA)
                    for m in range(MQK):
                        pe.wait_ge(full_ready, 2 * MQK * i + MQK * u + m + 1)
                        for k in range(KC):
                            mm = nc.tensor.matmul(qk_psum[:, m, :], w_qkv[:, k, m * P:(m + 1) * P],
                                                  xT[:, u, k, :], start=k == 0, stop=k == KC - 1)
                        mm.then_inc(qk_ready, 1)
                    pe.wait_ge(v_sb_ready, 2 * i + u + 1)
                    for s in range(SUB):
                        for k in range(KC):
                            mm = nc.tensor.matmul(v_psum[:, s // 2, s % 2, :], xT[:, u, k, s * P:(s + 1) * P],
                                                  w_qkv[:, k, 2 * C:3 * C], start=k == 0, stop=k == KC - 1)
                    mm.then_inc(v_ready, 1)

        @block.scalar
        def _(act):
            act.sem_inc(full_ready, MQK)
            act.wait_ge(bias_ready, 1)
            with act.Fori(0, NT // 2) as i:
                for u in range(2):
                    for m in range(MQK):
                        n = MQK * u + m
                        scale = SCALE if m < MQK // 2 else 1.0
                        act.wait_ge(qk_ready, 2 * MQK * i + n + 1)
                        act.wait_ge(parts_ready, 2 * MQK * i + n + 1)
                        act.wait_ge(parts_stored[m], 2 * DMA * i + DMA * u)
                        nc.scalar.activation(full[:, m % 2], qk_psum[:, m, :], ACT.Identity,
                                             bias=b_qk_scaled[:, m:m + 1], scale=scale)
                        nc.scalar.activation(parts[:, m, 0], qk_psum[:, m, :], ACT.Identity,
                                             bias=b_qk_scaled[:, m:m + 1], scale=scale).then_inc(full_ready, 1)

        @block.vector
        def _(dve):
            dve.sem_inc(parts_ready, 2)
            dve.sem_inc(v_sb_ready, 1)
            nc.vector.memset(v_ones[:], 1.0).then_inc(ones_ready, 1)
            dve.wait_ge(w_loaded, 3 * DMA)
            h = MQK // 2
            nc.vector.tensor_scalar_mul(b_qk_scaled[:, 0:h], b_qk[:, 0:h], SCALE)
            nc.vector.tensor_copy(b_qk_scaled[:, h:MQK], b_qk[:, h:MQK]).then_inc(bias_ready, 1)
            dve.wait_ge(ones_ready, 1)
            with dve.Fori(0, NT // 2) as i:
                for u in range(2):
                    for m in range(MQK):
                        n = MQK * u + m
                        dve.wait_ge(full_ready, 2 * MQK * i + n + 1 + MQK)
                        nc.vector.tensor_sub(rest[:, m % 2], full[:, m % 2], parts[:, m, 0]).then_inc(step_done, 1)
                        dve.wait_ge(step_done, 4 * MQK * i + 2 * n + 1)
                        nc.vector.tensor_copy(parts[:, m, 1], rest[:, m % 2]).then_inc(step_done, 1)
                        dve.wait_ge(step_done, 4 * MQK * i + 2 * n + 2)
                        nc.vector.tensor_sub(parts[:, m, 2], rest[:, m % 2], parts[:, m, 1]).then_inc(parts_ready, 1)
                    dve.wait_ge(v_ready, 2 * i + u + 3)
                    dve.wait_ge(v_stored[u], DMA * G * i)
                    for s in range(SUB):
                        add = nc.vector.tensor_add(
                            v_ones[:, u, s, :, :, 0, :].rearrange("p g j d -> p (g j) d"),
                            v_psum[:, s // 2, s % 2, :].rearrange("p (h d) -> p h d", d=D),
                            b_v[:].rearrange("p (h d) -> p h d", d=D))
                    add.then_inc(v_sb_ready, 1)

        @block.gpsimd
        def _(pool):
            part_dst = dram["parts"].rearrange("c (m p) (n t) -> n m p c t", p=P, t=TB)
            v_dst = dram["v_ones"].rearrange("g p (n s) e -> n g p s e", s=SUB)
            with pool.Fori(0, NT // 2) as i:
                for u in range(2):
                    for m in range(MQK):
                        pool.wait_ge(parts_ready, 2 * MQK * i + MQK * u + m + 3)
                        pool.sem_inc(waits_passed, 1)
                        pool.dma_start(part_dst[2 * i + u, m], parts[:, m]).then_inc(parts_stored[m], DMA)
                    pool.wait_ge(v_sb_ready, 2 * i + u + 2)
                    pool.sem_inc(waits_passed, 1)
                    for g in range(G):
                        pool.dma_start(v_dst[2 * i + u, g],
                                       v_ones[:, u, :, g].rearrange("p s j c d -> p s (j c d)")
                                       ).then_inc(v_stored[u], DMA)
            for m in range(MQK):
                pool.wait_ge(parts_stored[m], DMA * NT)
            for u in range(2):
                pool.wait_ge(v_stored[u], DMA * G * NT // 2)


def plan(NT, SUB):
    LEAD = 3
    steps = [(tb, sb) for tb in range(NT) for sb in range(SUB * (tb + 1))]
    first_step = [SUB * SUB * 0 + sum(SUB * (b + 1) for b in range(tb)) for tb in range(NT + 1)]
    chunks = [-(-(tb + 1) // 2) for tb in range(NT)]
    units = [(tb, u, j, c) for tb in range(NT) for c in range(chunks[tb]) for u in range(SUB) for j in range(4)]
    last_unit = [sum(16 * chunks[b] for b in range(tb + 1)) for tb in range(NT)]
    width = [min(8, SUB * tb + u + 1 - 8 * c) for tb, u, _, c in units]
    total = [0]
    for w in width:
        total.append(total[-1] + w)
    units_before = []
    for n in range(len(steps) + 1):
        tb = max([b for b in range(NT) if first_step[b] - LEAD <= n], default=0)
        if tb == NT - 1:
            units_before.append(len(units))
            continue
        a, b = first_step[tb] - LEAD, first_step[tb + 1] - LEAD
        done, due = total[last_unit[tb]], total[last_unit[tb + 1]]
        goal = done + (due - done) * (n - a) / (b - a)
        units_before.append(next(k for k in range(len(total)) if total[k] >= goal - 1e-9))
    return steps, first_step, chunks, units, last_unit, units_before


def attention(nc, dram, T, C, H):
    NT = T // TB
    NB = T // P
    SUB = TB // P
    D = C // H
    G = H // 4
    QK_ROWS = ALIBI + len(Q_PART) * D
    ROWS = QK_ROWS + 2
    steps, first_step, chunks, units, last_unit, units_before = plan(NT, SUB)
    NSTEP, NTILE, NUNIT = len(steps), 4 * len(steps), len(units) + NT
    SLOTS = 3
    PSLOTS = 12
    assert NTILE % SLOTS == 0 and NTILE % PSLOTS == 0 and NUNIT % 2 == 0 and ROWS <= P

    ring = []
    for k, unit in enumerate(units):
        for tb in range(NT):
            if k == last_unit[tb] + 2:
                ring.append(("turn", tb))
        ring.append(("unit", k))
    ring.append(("turn", NT - 1))
    place = {what: r for r, what in enumerate(ring)}
    ring_before = [place[("unit", k)] if k < len(units) else len(ring) for k in units_before]

    with ExitStack() as ctx:
        def sb(name, shape, dt):
            return ctx.enter_context(nc.sbuf_tensor(name, shape, dt))

        def ps(name, shape, dt):
            return ctx.enter_context(nc.psum_tensor(name, shape, dt))

        def sem(name):
            return ctx.enter_context(nc.semaphore(name))

        Qs = sb("Qs", [P, NT, 4, TB], BF16)
        Ks = sb("Ks", [P, NT, 4, TB], BF16)
        Vs = sb("Vs", [P, NB, 4, 2 * D], F32)
        probs = sb("probs", [P, PSLOTS, TB], F32)
        future = sb("future", [P, P], BF16)
        ident = sb("ident", [P, P], BF16)
        chunk_max = sb("chunk_max", [P, NT, 16, 4], F32)
        row_max = sb("row_max", [P, NT, 16], F32)
        neg_parts = sb("neg_parts", [P, NT, 2, 16], BF16)
        neg_rows = sb("neg_rows", [32, NT, P], BF16)
        acc = sb("acc", [P, 2, TB], F32)
        recip = sb("recip", [P, 2, TB], F32)
        recip_y = sb("recip_y", [P, 2, TB], F32)
        y_out = sb("y_out", [P, 2, TB], F32)

        max_psum = ps("max_psum", [P, 2, 2 * TB], F32)
        score_psum = ps("score_psum", [P, SLOTS, TB], F32)
        y_psum = ps("y_psum", [P, TB], F32)

        const_loaded = sem("const_loaded")
        q_loaded = [sem(f"q_loaded_{c}") for c in range(NT)]
        k_loaded = [sem(f"k_loaded_{c}") for c in range(NT)]
        v_loaded = [sem(f"v_loaded_{c}") for c in range(NT)]
        ring_ready = sem("ring_ready")
        ring_free = sem("ring_free")
        chunks_done = sem("chunks_done")
        small_done = sem("small_done")
        neg_ready = sem("neg_ready")
        neg_rows_ready = sem("neg_rows_ready")
        max_loaded = sem("max_loaded")
        scores_ready = sem("scores_ready")
        exp_done = sem("exp_done")
        pv_done = sem("pv_done")
        acc_copied = sem("acc_copied")
        norm_step = sem("norm_step")
        norm_ready = sem("norm_ready")
        y_ready = sem("y_ready")
        y_stored = [sem("y_stored_0"), sem("y_stored_1")]
        waits_passed = sem("waits_passed")
        block = ctx.enter_context(nc.Block())

        def load_q(sp, g, c):
            sp.dma_start(Qs[0:ALIBI, c], dram["alibi_q"].rearrange("(g j) r (n t) -> g n r j t", j=4, t=TB)[g, c]
                         ).then_inc(q_loaded[c], DMA)
            for n, part in enumerate(Q_PART):
                src = dram["parts"][part].rearrange("(a g j d) (n t) -> a g n d j t", a=2, j=4, d=D, t=TB)
                sp.dma_start(Qs[ALIBI + n * D:ALIBI + (n + 1) * D, c], src[0, g, c]).then_inc(q_loaded[c], DMA)

        def load_k(sp, g, c):
            for n, part in enumerate(K_PART):
                src = dram["parts"][part].rearrange("(a g j d) (n t) -> a g n d j t", a=2, j=4, d=D, t=TB)
                sp.dma_start(Ks[ALIBI + n * D:ALIBI + (n + 1) * D, c], src[1, g, c]).then_inc(k_loaded[c], DMA)

        def load_v(sp, g, c):
            sp.dma_start(Vs[:, SUB * c:SUB * (c + 1)].rearrange("p s j e -> p s (j e)"),
                         dram["v_ones"][g, :, SUB * c:SUB * (c + 1), :]).then_inc(v_loaded[c], DMA)

        Q_DMAS, K_DMAS = 1 + len(Q_PART), len(K_PART)

        @block.sync
        def _(sp):
            sp.dma_start(ident[:], dram["ident"]).then_inc(const_loaded, DMA)
            sp.dma_start(future[:], dram["future"]).then_inc(const_loaded, DMA)
            for j in range(4):
                sp.dma_start(Ks[0:ALIBI, :, j], dram["alibi_k"].rearrange("r (n t) -> r n t", t=TB)
                             ).then_inc(const_loaded, DMA)
                sp.dma_start(Ks[QK_ROWS:ROWS, :, j], dram["alibi_k"][2:4].rearrange("r (n t) -> r n t", t=TB)
                             ).then_inc(const_loaded, DMA)
            for c in range(NT):
                load_q(sp, 0, c)
                load_k(sp, 0, c)
                load_v(sp, 0, c)
            with sp.Fori(0, G - 1) as g:
                for c in range(NT):
                    sp.wait_ge(scores_ready, NTILE * g + 4 * first_step[c + 1])
                    load_q(sp, g + 1, c)
                for c in range(NT):
                    n = first_step[NT - 1] + SUB * (c + 1)
                    sp.wait_ge(scores_ready, NTILE * g + 4 * n)
                    load_k(sp, g + 1, c)
                    sp.wait_ge(pv_done, NSTEP * g + n + 3)
                    load_v(sp, g + 1, c)

        @block.tensor
        def _(pe):
            pe.sem_inc(pv_done, 3)
            pe.wait_ge(const_loaded, 10 * DMA)

            def max_unit(g, r):
                kind, k = ring[r]
                pe.wait_ge(ring_free, NUNIT * g + r + 1)
                if kind == "turn":
                    pe.wait_ge(neg_ready, NT * g + k + 1)
                    nc.tensor.transpose(max_psum[0:32, r % 2, 0:P // 2].bitcast(BF16),
                                        neg_parts[:, k].rearrange("p c n -> p (c n)"), ident[:]).then_inc(ring_ready, 1)
                    return
                tb, u, j, c = units[k]
                if k == 0 or units[k - 1][0] != tb:
                    pe.wait_ge(q_loaded[tb], Q_DMAS * DMA * g + Q_DMAS * DMA)
                    pe.wait_ge(k_loaded[tb], K_DMAS * DMA * g + K_DMAS * DMA)
                q_block = Qs[0:QK_ROWS, tb, j, u * P:(u + 1) * P]
                end = (SUB * tb + u + 1) * P
                for s in range(8 * P * c, min(8 * P * (c + 1), end), TB):
                    w = min(TB, end - s)
                    diag = s + w == end
                    out = max_psum[:, r % 2, s - 8 * P * c:s - 8 * P * c + w]
                    mm = nc.tensor.matmul(out, q_block, Ks[0:QK_ROWS, s // TB, j, 0:w], start=True, stop=not diag)
                    if diag:
                        mm = nc.tensor.matmul(out[:, w - P:w], ident[:], future[:], start=False, stop=True)
                mm.then_inc(ring_ready, 1)

            def score_tile(g, n, j):
                tb, s = steps[n]
                skip = max(0, s - SUB * tb) * P
                e = 4 * n + j
                out = score_psum[:, e % SLOTS, 0:TB - skip]
                diag = s >= SUB * tb
                pe.wait_ge(exp_done, NTILE * g + e + 1)
                mm = nc.tensor.matmul(out, Ks[0:ROWS, s // SUB, j, (s % SUB) * P:(s % SUB + 1) * P],
                                      Qs[0:ROWS, tb, j, skip:TB], start=True, stop=not diag)
                if diag:
                    mm = nc.tensor.matmul(out[:, 0:P], future[:], ident[:], start=False, stop=True)
                mm.then_inc(scores_ready, 1)

            def weigh(g, n):
                tb, s = steps[n]
                skip = max(0, s - SUB * tb) * P
                if s == 0:
                    pe.wait_ge(acc_copied, NT * g + tb + 1)
                if s == SUB * tb:
                    pe.wait_ge(v_loaded[tb], DMA * g + DMA)
                pe.wait_ge(exp_done, NTILE * g + 4 * n + 4 + SLOTS)
                for j in range(4):
                    mm = nc.tensor.matmul(y_psum[32 * j:32 * j + 32, skip:TB], Vs[:, s, j, :],
                                          probs[:, (4 * n + j) % PSLOTS, 0:TB - skip],
                                          start=s == 0, stop=s == SUB * (tb + 1) - 1)
                mm.then_inc(pv_done, 1)

            with pe.Fori(0, G) as g:
                for r in range(ring_before[0]):
                    max_unit(g, r)
                for n in range(NSTEP):
                    tb, s = steps[n]
                    a, b = ring_before[n], ring_before[n + 1]
                    mid = (a + b + 1) // 2
                    if s == 0:
                        pe.wait_ge(max_loaded, 2 * DMA * NT * g + 2 * DMA * (tb + 1))
                    score_tile(g, n, 0)
                    score_tile(g, n, 1)
                    for r in range(a, mid):
                        max_unit(g, r)
                    if n:
                        weigh(g, n - 1)
                    score_tile(g, n, 2)
                    for r in range(mid, b):
                        max_unit(g, r)
                    score_tile(g, n, 3)
                weigh(g, NSTEP - 1)

        @block.scalar
        def _(act):
            act.sem_inc(exp_done, SLOTS)
            act.sem_inc(acc_copied, 1)

            def take_sums(g, tb):
                act.wait_ge(pv_done, NSTEP * g + first_step[tb + 1] + 3)
                if tb >= 2:
                    act.wait_ge(y_ready, NT * g + tb - 1)
                else:
                    act.wait_ge(y_ready, NT * g)
                nc.scalar.activation(acc[:, tb % 2], y_psum[:], ACT.Copy).then_inc(acc_copied, 1)

            with act.Fori(0, G) as g:
                for n in range(NSTEP):
                    tb, s = steps[n]
                    skip = max(0, s - SUB * tb) * P
                    act.wait_ge(pv_done, NSTEP * g + n + 1)
                    for j in range(4):
                        e = 4 * n + j
                        act.wait_ge(scores_ready, NTILE * g + e + 1)
                        nc.scalar.activation(probs[:, e % PSLOTS, 0:TB - skip], score_psum[:, e % SLOTS, 0:TB - skip],
                                             ACT.Exp).then_inc(exp_done, 1)
                    if s == 0 and tb > 0:
                        take_sums(g, tb - 1)
                take_sums(g, NT - 1)

        @block.vector
        def _(dve):
            dve.sem_inc(ring_free, 2)

            def reduce_unit(g, r):
                kind, k = ring[r]
                dve.wait_ge(ring_ready, NUNIT * g + r + 1)
                if kind == "turn":
                    nc.vector.tensor_copy(neg_rows[:, k], max_psum[0:32, r % 2, 0:P // 2].bitcast(BF16)
                                          ).then_inc(neg_rows_ready, 1)
                    dve.wait_ge(neg_rows_ready, NT * g + k + 1)
                    dve.sem_inc(ring_free, 1)
                    return
                tb, u, j, c = units[k]
                w = min(8 * P, (SUB * tb + u + 1 - 8 * c) * P)
                nc.vector.reduce_max(chunk_max[:, tb, 4 * j + u, c:c + 1], max_psum[:, r % 2, 0:w], AX_X
                                     ).then_inc(ring_free, 1)
                if k + 1 == last_unit[tb]:
                    small = 2 * (NT * g + tb)
                    dve.wait_ge(ring_free, NUNIT * g + r + 3)
                    nc.vector.reduce_max(row_max[:, tb], chunk_max[:, tb, :, 0:chunks[tb]], AX_X
                                         ).then_inc(small_done, 1)
                    dve.wait_ge(small_done, small + 1)
                    nc.vector.tensor_scalar_mul(neg_parts[:, tb, 0], row_max[:, tb], -1.0).then_inc(small_done, 1)
                    dve.wait_ge(small_done, small + 2)
                    nc.vector.scalar_tensor_tensor(out=neg_parts[:, tb, 1], in0=row_max[:, tb], scalar=-1.0,
                                                   in1=neg_parts[:, tb, 0], op0=ALU.mult, op1=ALU.subtract
                                                   ).then_inc(neg_ready, 1)

            def norm(g, tb):
                dve.wait_ge(acc_copied, NT * g + tb + 2)
                nc.vector.reciprocal(recip[:, tb % 2], acc[:, tb % 2]).then_inc(norm_step, 1)
                dve.wait_ge(norm_step, NT * g + tb + 1)
                dve.sem_inc(waits_passed, 1)
                nc.vector.stream_shuffle(recip_y[:, tb % 2], recip[:, tb % 2],
                                         [D + i % D for i in range(32)]).then_inc(norm_ready, 1)

            with dve.Fori(0, G) as g:
                for r in range(ring_before[0]):
                    reduce_unit(g, r)
                for n in range(NSTEP):
                    tb, s = steps[n]
                    for r in range(ring_before[n], ring_before[n + 1]):
                        reduce_unit(g, r)
                    if s == 1 and tb > 0:
                        norm(g, tb - 1)
                norm(g, NT - 1)

        @block.gpsimd
        def _(pool):
            y_dst = dram["yT"].rearrange("g p (n t) -> g n p t", t=TB)

            def send_max(g, tb):
                pool.wait_ge(neg_rows_ready, NT * g + tb + 1)
                pool.sem_inc(waits_passed, 1)
                for part in range(2):
                    pool.dma_start(Qs[QK_ROWS + part:QK_ROWS + part + 1, tb].rearrange("p j t -> p (j t)"),
                                   neg_rows[16 * part:16 * part + 16, tb]).then_inc(max_loaded, DMA)

            def scale_y(g, tb):
                pool.wait_ge(norm_ready, NT * g + tb + 1)
                pool.wait_ge(y_stored[tb % 2], DMA * (NT // 2) * g + DMA * (tb // 2))
                nc.gpsimd.tensor_tensor(y_out[:, tb % 2], acc[:, tb % 2], recip_y[:, tb % 2], ALU.mult
                                        ).then_inc(y_ready, 1)
                pool.wait_ge(y_ready, NT * g + tb + 1)
                pool.sem_inc(waits_passed, 1)
                pool.dma_start(y_dst[g, tb], y_out[:, tb % 2]).then_inc(y_stored[tb % 2], DMA)

            with pool.Fori(0, G) as g:
                send_max(g, 0)
                for tb in range(1, NT):
                    send_max(g, tb)
                    scale_y(g, tb - 1)
                scale_y(g, NT - 1)
            for b in range(2):
                pool.wait_ge(y_stored[b], DMA * G * NT // 2)


def ffn(nc, dram, T, C, H, F):
    NT = T // TB
    SUB = TB // P
    KC = C // P
    KF = F // P
    G = H // 4
    D = C // H

    with ExitStack() as ctx:
        def sb(name, shape, dt):
            return ctx.enter_context(nc.sbuf_tensor(name, shape, dt))

        def ps(name, shape, dt):
            return ctx.enter_context(nc.psum_tensor(name, shape, dt))

        def sem(name):
            return ctx.enter_context(nc.semaphore(name))

        w_proj = sb("w_proj", [P, G, C], F32)
        b_proj = sb("b_proj", [P, C], F32)
        w1 = sb("w1", [P, KC, F], F32)
        w2 = sb("w2", [P, KC, F], F32)
        w3 = sb("w3", [P, KF, F], F32)
        w4 = sb("w4", [P, KF, F], F32)
        w5 = sb("w5", [P, KF, C], F32)
        scales = sb("scales", [P, 4, KF], F32)
        s5 = sb("s5", [P, C], F32)
        ident = sb("ident_f", [P, P], F32)
        minus_half = sb("minus_half", [P, SUB], F32)
        yT = sb("yT", [P, G, TB], F32)
        x = sb("x", [P, SUB, C], F32)
        z = sb("z", [P, SUB, C], F32)
        x1 = sb("x1", [P, SUB, C], F32)
        out_sb = sb("out_sb", [P, SUB, C], F32)
        x1T = sb("x1T", [P, KC, TB], F32)
        gate = sb("gate", [P, 2, TB], F32)
        hid = sb("hid", [P, 2, KF, TB], F32)
        stats = sb("stats", [P, SUB, 6], F32)
        moments = sb("moments", [P, SUB, 2], F32)
        var_eps = sb("var_eps", [P, SUB], F32)
        rstd = sb("rstd", [P, SUB], F32)
        row_psum = ps("row_psum", [P, 2, TB], F32)
        hid_psum = ps("hid_psum", [P, 4, TB], F32)

        w_loaded = sem("w_loaded_f")
        zeroed = sem("zeroed")
        y_loaded = sem("y_loaded")
        x_loaded = sem("x_loaded_f")
        proj_ready = sem("proj_ready")
        z_ready = sem("z_ready")
        stat_step = sem("stat_step")
        var_ready = sem("var_ready")
        rstd_ready = sem("rstd_ready")
        x1_ready = sem("x1_ready")
        turned = sem("turned")
        x1T_ready = sem("x1T_ready")
        hid_ready = sem("hid_ready")
        gate_ready = sem("gate_ready")
        up_ready = sem("up_ready")
        gelu_ready = sem("gelu_ready")
        down_ready = sem("down_ready")
        z2_ready = sem("z2_ready")
        sum_step = sem("sum_step")
        out_ready = sem("out_ready")
        out_stored = sem("out_stored")
        waits_passed = sem("waits_passed")
        block = ctx.enter_context(nc.Block())
        HT = 4 * KF
        W_DMAS = 4 + 1 + 5 + 2 + 1

        @block.sync
        def _(sp):
            sp.wait_ge(zeroed, 1)
            for j in range(4):
                sp.dma_start(w_proj[32 * j:32 * j + D], dram["w_proj"].rearrange("(g j d) n -> j d g n", j=4, d=D)[j]
                             ).then_inc(w_loaded, DMA)
            sp.dma_start(b_proj[:], dram["b_proj"]).then_inc(w_loaded, DMA)
            sp.dma_start(ident[:], dram["ident_f"]).then_inc(w_loaded, DMA)
            for w, name in ((w1, "w1T"), (w2, "w2T"), (w3, "h1T"), (w4, "h2T"), (w5, "w3T")):
                sp.dma_start(w[:], dram[name].rearrange("(k p) n -> p k n", p=P)).then_inc(w_loaded, DMA)
            sp.dma_start(scales[:], dram["scales"]).then_inc(w_loaded, DMA)
            sp.dma_start(s5[:], dram["s5"]).then_inc(w_loaded, DMA)
            with sp.Fori(0, NT) as i:
                sp.wait_ge(proj_ready, SUB * i)
                sp.dma_start(yT[:], dram["yT"].rearrange("g p (n t) -> n p g t", t=TB)[i]).then_inc(y_loaded, DMA)
                sp.wait_ge(z_ready, SUB * i)
                sp.dma_start(x[:], dram["x"].rearrange("(n s p) c -> n p s c", s=SUB, p=P)[i]).then_inc(x_loaded, DMA)

        @block.gpsimd
        def _(pool):
            nc.gpsimd.memset(minus_half[:], -0.5)
            nc.gpsimd.memset(w_proj[:], 0.0).then_inc(zeroed, 1)
            pool.wait_ge(zeroed, 1)
            dst = dram["out"].rearrange("(n s p) c -> n p s c", s=SUB, p=P)
            with pool.Fori(0, NT) as i:
                for half in range(2):
                    pool.wait_ge(var_ready, 2 * i + half + 1)
                    nc.gpsimd.tensor_tensor(rstd[:], var_eps[:], minus_half[:], ALU.pow).then_inc(rstd_ready, 1)
                pool.wait_ge(out_ready, SUB * i + SUB)
                pool.sem_inc(waits_passed, 1)
                pool.dma_start(dst[i], out_sb[:]).then_inc(out_stored, DMA)
            pool.wait_ge(out_stored, DMA * NT)

        @block.tensor
        def _(pe):
            pe.wait_ge(w_loaded, W_DMAS * DMA)
            with pe.Fori(0, NT) as i:
                pe.wait_ge(y_loaded, DMA * i + DMA)
                for s in range(SUB):
                    if s >= 2:
                        pe.wait_ge(z_ready, SUB * i + s - 1)
                    else:
                        pe.wait_ge(z2_ready, SUB * i)
                    for g in range(G):
                        mm = nc.tensor.matmul(row_psum[:, s % 2, 0:C], yT[:, g, s * P:(s + 1) * P], w_proj[:, g, :],
                                              start=g == 0, stop=g == G - 1)
                    mm.then_inc(proj_ready, 1)
                pe.wait_ge(z_ready, SUB * i + SUB)
                for s in range(SUB):
                    pe.wait_ge(x1_ready, SUB * i + s + 1)
                    for k in range(KC):
                        mm = nc.tensor.transpose(row_psum[:, k, s * P:(s + 1) * P], x1[:, s, k * P:(k + 1) * P], ident[:])
                mm.then_inc(turned, 1)
                pe.wait_ge(x1T_ready, KC * i + KC)
                for m in range(KF):
                    for t, w in enumerate((w1, w2)):
                        n = 2 * m + t
                        if m >= 2:
                            pe.wait_ge(up_ready, KF * i + m - 1)
                        else:
                            pe.wait_ge(gelu_ready, 2 * KF * i)
                        for k in range(KC):
                            mm = nc.tensor.matmul(hid_psum[:, n % 4, :], w[:, k, m * P:(m + 1) * P], x1T[:, k, :],
                                                  start=k == 0, stop=k == KC - 1)
                        mm.then_inc(hid_ready, 1)
                for lay, w in enumerate((w3, w4)):
                    src = hid[:, lay]
                    for m in range(KF):
                        n = 2 * KF + KF * lay + m
                        if lay == 0 and m == 0:
                            pe.wait_ge(up_ready, KF * i + KF - 1)
                        elif lay == 1 or m >= 4:
                            pe.wait_ge(gelu_ready, 2 * KF * i + KF * lay + m - 3)
                        for k in range(KF):
                            if m == 0 and lay == 0:
                                pe.wait_ge(up_ready, KF * i + k + 1)
                            if m == 0 and lay == 1:
                                pe.wait_ge(gelu_ready, 2 * KF * i + k + 1)
                            mm = nc.tensor.matmul(hid_psum[:, n % 4, :], w[:, k, m * P:(m + 1) * P], src[:, k, :],
                                                  start=k == 0, stop=k == KF - 1)
                        mm.then_inc(hid_ready, 1)
                for s in range(SUB):
                    if s >= 2:
                        pe.wait_ge(z2_ready, SUB * i + s - 1)
                    for k in range(KF):
                        if s == 0:
                            pe.wait_ge(gelu_ready, 2 * KF * i + KF + k + 1)
                        mm = nc.tensor.matmul(row_psum[:, s % 2, 0:C], hid[:, 0, k, s * P:(s + 1) * P], w5[:, k, :],
                                              start=k == 0, stop=k == KF - 1)
                    mm.then_inc(down_ready, 1)

        @block.scalar
        def _(act):
            act.wait_ge(w_loaded, W_DMAS * DMA)
            with act.Fori(0, NT) as i:
                act.wait_ge(turned, i + 1)
                for k in range(KC):
                    nc.scalar.activation(x1T[:, k], row_psum[:, k], ACT.Copy).then_inc(x1T_ready, 1)
                for m in range(KF):
                    act.wait_ge(hid_ready, HT * i + 2 * m + 1)
                    if m >= 2:
                        act.wait_ge(up_ready, KF * i + m - 1)
                    else:
                        act.wait_ge(up_ready, KF * i)
                    nc.scalar.activation(gate[:, m % 2], hid_psum[:, (2 * m) % 4], ACT.Silu,
                                         scale=scales[:, 0, m:m + 1]).then_inc(gate_ready, 1)
                for lay in range(2):
                    for m in range(KF):
                        n = 2 * KF + KF * lay + m
                        act.wait_ge(hid_ready, HT * i + n + 1)
                        nc.scalar.activation(hid[:, 1 - lay, m], hid_psum[:, n % 4], ACT.Gelu,
                                             scale=scales[:, 2 + lay, m:m + 1]).then_inc(gelu_ready, 1)

        @block.vector
        def _(dve):
            dve.wait_ge(w_loaded, W_DMAS * DMA)
            with dve.Fori(0, NT) as i:
                def layer_norm(src, dst, ready, half):
                    base = 2 * SUB * 2 * i + 2 * SUB * half
                    for s in range(SUB):
                        nc.vector.bn_stats(stats[:, s], src[:, s]).then_inc(stat_step, 1)
                    dve.wait_ge(stat_step, base + SUB)
                    dve.sem_inc(waits_passed, 1)
                    for s in range(SUB):
                        nc.vector.bn_aggr(moments[:, s], stats[:, s]).then_inc(stat_step, 1)
                    dve.wait_ge(stat_step, base + 2 * SUB)
                    nc.vector.tensor_scalar_add(var_eps[:], moments[:, :, 1], EPS).then_inc(var_ready, 1)
                    dve.wait_ge(rstd_ready, 2 * i + half + 1)
                    for s in range(SUB):
                        nc.vector.tensor_scalar(dst[:, s], src[:, s], moments[:, s, 0:1], rstd[:, s:s + 1],
                                                ALU.subtract, ALU.mult).then_inc(ready, 1)

                dve.wait_ge(x_loaded, DMA * i + DMA)
                dve.wait_ge(out_ready, SUB * i)
                for s in range(SUB):
                    add = nc.vector.tensor_add(z[:, s], x[:, s], b_proj[:])
                add.then_inc(sum_step, 1)
                dve.wait_ge(sum_step, 2 * i + 1)
                for s in range(SUB):
                    dve.wait_ge(proj_ready, SUB * i + s + 1)
                    nc.vector.tensor_add(z[:, s], z[:, s], row_psum[:, s % 2, 0:C]).then_inc(z_ready, 1)
                dve.wait_ge(z_ready, SUB * i + SUB)
                layer_norm(z, x1, x1_ready, 0)
                for m in range(KF):
                    dve.wait_ge(gate_ready, KF * i + m + 1)
                    dve.wait_ge(hid_ready, HT * i + 2 * m + 2)
                    nc.vector.scalar_tensor_tensor(out=hid[:, 0, m], in0=hid_psum[:, (2 * m + 1) % 4],
                                                   scalar=scales[:, 1, m:m + 1], in1=gate[:, m % 2],
                                                   op0=ALU.mult, op1=ALU.mult).then_inc(up_ready, 1)
                for s in range(SUB):
                    dve.wait_ge(down_ready, SUB * i + s + 1)
                    nc.vector.tensor_mul(z[:, s], row_psum[:, s % 2, 0:C], s5[:]).then_inc(z2_ready, 1)
                dve.wait_ge(z2_ready, SUB * i + SUB)
                for s in range(SUB):
                    add = nc.vector.tensor_add(z[:, s], z[:, s], x1[:, s])
                add.then_inc(sum_step, 1)
                dve.wait_ge(sum_step, 2 * i + 2)
                dve.wait_ge(out_stored, DMA * i)
                layer_norm(z, out_sb, out_ready, 1)


def build(nc, dram, T, C, H, F):
    project(nc, dram, T, C, H)
    attention(nc, dram, T, C, H)
    ffn(nc, dram, T, C, H, F)


def kernel(**inputs):
    import numpy as np
    import concourse.bacc as bacc
    from concourse import mybir as _mybir
    from concourse.bass_utils import run_bass_kernel_spmd

    x = np.ascontiguousarray(inputs["L0_attn_x"])[0]
    T, C = x.shape
    H = 16
    F = inputs["L0_ffn_w1_w"].shape[0]
    w_attn = np.ascontiguousarray(inputs["L0_attn_W_attn"])
    b_attn = np.ascontiguousarray(inputs["L0_attn_b_attn"])

    def bf16_bits(a):
        return (np.ascontiguousarray(a, dtype=np.float32).view(np.uint32) >> 16).astype(np.uint16)

    def rows(v):
        return np.ascontiguousarray(np.broadcast_to(v, (128, v.shape[0])))

    def columns(v):
        return np.ascontiguousarray(np.asarray(v).reshape(-1, 128).T)

    pos = np.arange(T)
    slope = 0.5 ** np.arange(1, H + 1)[:, None]
    alibi_k = np.stack([pos % 128, pos - pos % 128, np.ones(T), np.ones(T)])
    alibi_q = np.stack([slope + 0 * pos, slope + 0 * pos, -slope * (pos % 128), -slope * (pos - pos % 128)], axis=1)
    future = np.where(np.arange(128)[None, :] > np.arange(128)[:, None], -1e30, 0.0)
    arrays = {
        "x": x,
        "xT": np.ascontiguousarray(x.T),
        "w_attn": w_attn,
        "b_qk": columns(b_attn[:2 * C]),
        "b_v": rows(b_attn[2 * C:]),
        "w_proj": np.ascontiguousarray(inputs["L0_attn_W_proj"]),
        "b_proj": rows(np.asarray(inputs["L0_attn_b_proj"])),
        "w1T": np.ascontiguousarray(np.asarray(inputs["L0_ffn_w1_w"]).T),
        "w2T": np.ascontiguousarray(np.asarray(inputs["L0_ffn_w2_w"]).T),
        "h1T": np.ascontiguousarray(np.asarray(inputs["L0_ffn_h1_w"]).T),
        "h2T": np.ascontiguousarray(np.asarray(inputs["L0_ffn_h2_w"]).T),
        "w3T": np.ascontiguousarray(np.asarray(inputs["L0_ffn_w3_w"]).T),
        "scales": np.ascontiguousarray(np.stack([columns(inputs[f"L0_ffn_{n}_s"]) for n in ("w1", "w2", "h1", "h2")], 1)),
        "s5": rows(np.asarray(inputs["L0_ffn_w3_s"])),
        "ident_f": np.eye(128, dtype=np.float32),
        "ident": bf16_bits(np.eye(128)),
        "future": bf16_bits(future),
        "alibi_k": bf16_bits(alibi_k),
        "alibi_q": bf16_bits(alibi_q),
    }
    nc = bacc.Bacc("TRN2", target_bir_lowering=False, num_devices=1)
    dram = {}
    for name, a in arrays.items():
        ap = nc.dram_tensor(name + "_dram", a.shape, _mybir.dt.from_np(a.dtype), kind="ExternalInput").ap()
        dram[name] = ap.bitcast(_mybir.dt.bfloat16) if a.dtype == np.uint16 else ap
    dram["parts"] = nc.dram_tensor("parts_dram", (3, 2 * C, T), _mybir.dt.bfloat16, kind="Internal").ap()
    dram["v_ones"] = nc.dram_tensor("v_ones_dram", (H // 4, 128, T // 128, 128), _mybir.dt.float32, kind="Internal").ap()
    dram["yT"] = nc.dram_tensor("yT_dram", (H // 4, 128, T), _mybir.dt.float32, kind="Internal").ap()
    dram["out"] = nc.dram_tensor("out_dram", (T, C), _mybir.dt.float32, kind="ExternalOutput").ap()
    build(nc, dram, T, C, H, F)
    r = run_bass_kernel_spmd(nc, [{k + "_dram": v for k, v in arrays.items()}], core_ids=[0])
    return r.results[0]["out_dram"].reshape(1, T, C)
```

```python
from contextlib import ExitStack

import concourse.bass as bass
from concourse import mybir

ALU = mybir.AluOpType
ACT = mybir.ActivationFunctionType
F32 = mybir.dt.float32
F32R = mybir.dt.float32r
I32 = mybir.dt.int32
BF16 = mybir.dt.bfloat16
U16 = mybir.dt.uint16
AX_X = mybir.AxisListType.X

P = 128
TB = 512
DMA = 16
EPS = 1e-5

Q_PART = (0, 0, 1, 0, 2, 1)
K_PART = (0, 1, 0, 2, 0, 1)
ALIBI = 4

PROJECT_AFTER = (0, 3)
TRANSPOSE_AFTER = (1, 1)
BEYOND_F32R = 0xFFF


def project(nc, dram, T, C, H):
    NT = T // TB
    KC = C // P
    MQK = 2 * C // P
    SUB = TB // P
    D = C // H
    G = H // 4
    SCALE = float(D) ** -0.5
    assert NT % 2 == 0 and 2 * D == 32

    with ExitStack() as ctx:
        def sb(name, shape, dt):
            return ctx.enter_context(nc.sbuf_tensor(name, shape, dt))

        def sem(name):
            return ctx.enter_context(nc.semaphore(name))

        xT = sb("xT", [P, 2, KC, TB], F32)
        w_qkv = sb("w_qkv", [P, KC, 3 * C], F32)
        b_qk = sb("b_qk", [P, MQK], F32)
        b_qk_scaled = sb("b_qk_scaled", [P, MQK], F32)
        b_v = sb("b_v", [P, C], F32)
        full = sb("full", [P, 2, TB], F32)
        rest = sb("rest", [P, 2, TB], F32)
        parts = sb("parts", [P, 4, 3, TB], BF16)
        v_ones = sb("v_ones", [P, 2, SUB, G, 4, 2, D], F32)
        qk_psum = ctx.enter_context(nc.psum_tensor("qk_psum", [P, MQK, TB], F32))
        v_psum = ctx.enter_context(nc.psum_tensor("v_psum", [P, SUB // 2, 2, C], F32))

        w_loaded = sem("w_loaded")
        x_loaded = [sem("x_loaded_0"), sem("x_loaded_1")]
        bias_ready = sem("bias_ready")
        ones_ready = sem("ones_ready")
        qk_ready = sem("qk_ready")
        v_ready = sem("v_ready")
        full_ready = sem("full_ready")
        step_done = sem("step_done")
        parts_ready = sem("parts_ready")
        parts_stored = [sem(f"parts_stored_{i}") for i in range(4)]
        v_sb_ready = sem("v_sb_ready")
        v_stored = [sem("v_stored_0"), sem("v_stored_1")]
        waits_passed = sem("waits_passed")
        block = ctx.enter_context(nc.Block())

        @block.sync
        def _(sp):
            sp.dma_start(w_qkv[:], dram["w_attn"].rearrange("(k p) n -> p k n", p=P)).then_inc(w_loaded, DMA)
            sp.dma_start(b_qk[:], dram["b_qk"]).then_inc(w_loaded, DMA)
            sp.dma_start(b_v[:], dram["b_v"]).then_inc(w_loaded, DMA)
            for stored in (*parts_stored, *v_stored):
                sp.sem_inc(stored, 1)
            part_dst = dram["parts"].rearrange("c (m p) (n t) -> n m p c t", p=P, t=TB)
            v_dst = dram["v_ones"].rearrange("g p (n s) e -> n g p s e", s=SUB)
            with sp.Fori(0, NT // 2) as i:
                for u in range(2):
                    for m in range(MQK):
                        sp.wait_ge(parts_ready, 2 * MQK * i + MQK * u + m + 3)
                        sp.sem_inc(waits_passed, 1)
                        sp.dma_start(part_dst[2 * i + u, m], parts[:, m]).then_inc(parts_stored[m], DMA)
                    sp.wait_ge(v_sb_ready, 2 * i + u + 2)
                    sp.sem_inc(waits_passed, 1)
                    for g in range(G):
                        sp.dma_start(v_dst[2 * i + u, g],
                                     v_ones[:, u, :, g].rearrange("p s j c d -> p s (j c d)")
                                     ).then_inc(v_stored[u], DMA)
            for m in range(MQK):
                sp.wait_ge(parts_stored[m], DMA * NT + 1)
            for u in range(2):
                sp.wait_ge(v_stored[u], DMA * G * NT // 2 + 1)

        @block.tensor
        def _(pe):
            pe.sem_inc(v_ready, 2)
            pe.wait_ge(w_loaded, 3 * DMA)
            with pe.Fori(0, NT // 2) as i:
                for u in range(2):
                    pe.wait_ge(x_loaded[u], DMA * i + DMA)
                    for m in range(MQK):
                        pe.wait_ge(full_ready, 2 * MQK * i + MQK * u + m + 1)
                        for k in range(KC):
                            mm = nc.tensor.matmul(qk_psum[:, m, :], w_qkv[:, k, m * P:(m + 1) * P],
                                                  xT[:, u, k, :], start=k == 0, stop=k == KC - 1)
                        mm.then_inc(qk_ready, 1)
                    pe.wait_ge(v_sb_ready, 2 * i + u + 1)
                    for s in range(SUB):
                        for k in range(KC):
                            mm = nc.tensor.matmul(v_psum[:, s // 2, s % 2, :], xT[:, u, k, s * P:(s + 1) * P],
                                                  w_qkv[:, k, 2 * C:3 * C], start=k == 0, stop=k == KC - 1)
                    mm.then_inc(v_ready, 1)

        @block.scalar
        def _(act):
            act.sem_inc(full_ready, MQK)
            act.wait_ge(bias_ready, 1)
            with act.Fori(0, NT // 2) as i:
                for u in range(2):
                    for m in range(MQK):
                        n = MQK * u + m
                        scale = SCALE if m < MQK // 2 else 1.0
                        act.wait_ge(qk_ready, 2 * MQK * i + n + 1)
                        act.wait_ge(parts_ready, 2 * MQK * i + n + 1)
                        act.wait_ge(parts_stored[m], 2 * DMA * i + DMA * u + 1)
                        nc.scalar.activation(full[:, m % 2], qk_psum[:, m, :], ACT.Identity,
                                             bias=b_qk_scaled[:, m:m + 1], scale=scale)
                        nc.scalar.activation(parts[:, m, 0], qk_psum[:, m, :], ACT.Identity,
                                             bias=b_qk_scaled[:, m:m + 1], scale=scale).then_inc(full_ready, 1)

        @block.vector
        def _(dve):
            dve.sem_inc(parts_ready, 2)
            dve.sem_inc(v_sb_ready, 1)
            nc.vector.memset(v_ones[:], 1.0).then_inc(ones_ready, 1)
            dve.wait_ge(w_loaded, 3 * DMA)
            h = MQK // 2
            nc.vector.tensor_scalar_mul(b_qk_scaled[:, 0:h], b_qk[:, 0:h], SCALE)
            nc.vector.tensor_copy(b_qk_scaled[:, h:MQK], b_qk[:, h:MQK]).then_inc(bias_ready, 1)
            dve.wait_ge(ones_ready, 1)
            with dve.Fori(0, NT // 2) as i:
                for u in range(2):
                    for m in range(MQK):
                        n = MQK * u + m
                        dve.wait_ge(full_ready, 2 * MQK * i + n + 1 + MQK)
                        nc.vector.tensor_sub(rest[:, m % 2], full[:, m % 2], parts[:, m, 0]).then_inc(step_done, 1)
                        dve.wait_ge(step_done, 4 * MQK * i + 2 * n + 1)
                        nc.vector.tensor_copy(parts[:, m, 1], rest[:, m % 2]).then_inc(step_done, 1)
                        dve.wait_ge(step_done, 4 * MQK * i + 2 * n + 2)
                        nc.vector.tensor_sub(parts[:, m, 2], rest[:, m % 2], parts[:, m, 1]).then_inc(parts_ready, 1)
                    dve.wait_ge(v_ready, 2 * i + u + 3)
                    dve.wait_ge(v_stored[u], DMA * G * i + 1)
                    for s in range(SUB):
                        add = nc.vector.tensor_add(
                            v_ones[:, u, s, :, :, 0, :].rearrange("p g j d -> p (g j) d"),
                            v_psum[:, s // 2, s % 2, :].rearrange("p (h d) -> p h d", d=D),
                            b_v[:].rearrange("p (h d) -> p h d", d=D))
                    add.then_inc(v_sb_ready, 1)

        @block.gpsimd
        def _(pool):
            x_src = dram["xT"].rearrange("(k p) (n t) -> n p k t", p=P, t=TB)
            with pool.Fori(0, NT // 2) as i:
                for u in range(2):
                    pool.wait_ge(v_ready, 2 * i + u + 1)
                    pool.sem_inc(waits_passed, 1)
                    pool.dma_start(xT[:, u], x_src[2 * i + u]).then_inc(x_loaded[u], DMA)


def plan(NT, SUB):
    LEAD = 3
    steps = [(p, tb, s) for p in range(2) for tb in range(NT) for s in range(SUB * (tb + 1))]
    first_step = [n for n, (_, _, s) in enumerate(steps) if s == 0] + [len(steps)]
    chunks = [-(-SUB * (tb + 1) // 8) for tb in range(NT)]
    ring, unit_left = [], []
    late = []
    for p in range(2):
        for tb in range(NT):
            for c in range(chunks[tb]):
                for u in range(SUB):
                    blocks = min(8, SUB * tb + u + 1 - 8 * c)
                    heads = 4 if blocks <= 2 else 2 if blocks <= 4 else 1
                    for j in range(0, 4, heads):
                        if late and late[0][0] == len(ring):
                            ring.append(("turn", late.pop(0)[1]))
                        last = (c, u, j + heads) == (chunks[tb] - 1, SUB - 1, 4)
                        ring.append(("unit", (p, tb, u, j, heads, c, blocks, last)))
            late.append((len(ring) + 3, NT * p + tb))
    ring.append(("turn", late.pop(0)[1]))
    keys = [0]
    for kind, what in ring:
        keys.append(keys[-1] + (what[4] * what[6] if kind == "unit" else 0))
    due = [(4 * (first_step[k] - LEAD), ring.index(("turn", k)) + 1) for k in range(2 * NT)]
    ring_at, r, done = [], 0, 0.0
    for quarter in range(4 * len(steps)):
        start = r
        r = max([r] + [entries for at, entries in due if at <= quarter])
        ahead = [(keys[entries] - max(done, keys[start])) / (at - quarter) for at, entries in due if at > quarter]
        done = max(done, keys[r]) + max(ahead, default=0.0)
        while r < len(ring) and keys[r + 1] <= done + 1e-6:
            r += 1
        ring_at.append(range(start, r))
    if len(ring) % 2:
        ring.append(("none", 0))
        ring_at[-1] = range(ring_at[-1].start, len(ring))
    assert ring_at[-1].stop == len(ring)
    return steps, first_step, chunks, ring, ring_at


def attention(nc, dram, T, C, H, F, seen_bits, w_early, early_loaded):
    NT = T // TB
    NB = T // P
    SUB = TB // P
    D = C // H
    G = H // 4
    QK_ROWS = ALIBI + len(Q_PART) * D
    ROWS = QK_ROWS + 2
    steps, first_step, chunks, ring, ring_at = plan(NT, SUB)
    NSTEP, NTILE, NRING, NTB = len(steps), 4 * len(steps), len(ring), 2 * NT
    SLOTS = 3
    PSLOTS = 12
    LAG = 2
    assert NTILE % SLOTS == 0 and NTILE % PSLOTS == 0 and NRING % 2 == 0 and ROWS <= P

    with ExitStack() as ctx:
        def sb(name, shape, dt):
            return ctx.enter_context(nc.sbuf_tensor(name, shape, dt))

        def ps(name, shape, dt):
            return ctx.enter_context(nc.psum_tensor(name, shape, dt))

        def sem(name):
            return ctx.enter_context(nc.semaphore(name))

        Qs = sb("Qs", [P, NT, 4, TB], BF16)
        Ks = sb("Ks", [P, 2, NT, 4, TB], BF16)
        Vs = sb("Vs", [P, NB, 4, 2 * D], F32)
        probs = sb("probs", [P, PSLOTS, TB], F32)
        future = sb("future", [P, P], BF16)
        ident = sb("ident", [P, P], BF16)
        chunk_max = sb("chunk_max", [P, NT, 4, SUB, chunks[-1]], F32)
        row_max = sb("row_max", [P, NT, 4, SUB], F32)
        neg_parts = sb("neg_parts", [P, NT, 2, 4, SUB], BF16)
        neg_rows = sb("neg_rows", [32, NT, P], BF16)
        acc = sb("acc", [P, 2, TB], F32)
        recip = sb("recip", [P, 2, TB], F32)
        recip_y = sb("recip_y", [P, 2, TB], F32)
        y_out = sb("y_out", [P, 2, TB], F32)
        w_stage = sb("w_stage", [P, F], F32)

        max_psum = ps("max_psum", [P, 2, 2 * TB], F32)
        score_psum = ps("score_psum", [P, SLOTS, TB], F32)
        y_psum = ps("y_psum", [P, TB], F32)

        const_loaded = sem("const_loaded")
        q_loaded = [sem(f"q_loaded_{c}") for c in range(NT)]
        k_loaded = [[sem(f"k_loaded_{p}_{c}") for c in range(NT)] for p in range(2)]
        v_loaded = [sem(f"v_loaded_{c}") for c in range(NT)]
        ring_ready = sem("ring_ready")
        ring_free = sem("ring_free")
        small_done = sem("small_done")
        neg_ready = sem("neg_ready")
        neg_rows_ready = sem("neg_rows_ready")
        max_loaded = sem("max_loaded")
        scores_ready = sem("scores_ready")
        exp_done = sem("exp_done")
        pv_done = sem("pv_done")
        acc_copied = sem("acc_copied")
        norm_step = sem("norm_step")
        norm_ready = sem("norm_ready")
        y_ready = sem("y_ready")
        y_stored = [sem("y_stored_0"), sem("y_stored_1")]
        seen_step = sem("seen_step")
        chunk_loaded = sem("chunk_loaded")
        chunk_stored = sem("chunk_stored")
        waits_passed = sem("waits_passed")
        block = ctx.enter_context(nc.Block())

        def load_q(sp, g, c):
            sp.dma_start(Qs[0:ALIBI, c], dram["alibi_q"].rearrange("(g j) r (n t) -> g n r j t", j=4, t=TB)[g, c]
                         ).then_inc(q_loaded[c], DMA)
            for n, part in enumerate(Q_PART):
                src = dram["parts"][part].rearrange("(a g j d) (n t) -> a g n d j t", a=2, j=4, d=D, t=TB)
                sp.dma_start(Qs[ALIBI + n * D:ALIBI + (n + 1) * D, c], src[0, g, c]).then_inc(q_loaded[c], DMA)

        def load_k(sp, g, p, c):
            for n, part in enumerate(K_PART):
                src = dram["parts"][part].rearrange("(a g j d) (n t) -> a g n d j t", a=2, j=4, d=D, t=TB)
                sp.dma_start(Ks[ALIBI + n * D:ALIBI + (n + 1) * D, p, c], src[1, g, c]).then_inc(k_loaded[p][c], DMA)

        def load_v(sp, g, c):
            sp.dma_start(Vs[:, SUB * c:SUB * (c + 1)].rearrange("p s j e -> p s (j e)"),
                         dram["v_ones"][g, :, SUB * c:SUB * (c + 1), :]).then_inc(v_loaded[c], DMA)

        Q_DMAS, K_DMAS = 1 + len(Q_PART), len(K_PART)
        CONST_DMAS = 2 + 4 * 2 * 2
        CHUNKS = dram["ffn_w"].shape[0] // (G // 2)
        quiet = [k for k in range(NTB) if k % NT >= 2][:CHUNKS]
        assert len(quiet) == CHUNKS and CHUNKS * (G // 2) == dram["ffn_w"].shape[0]

        @block.sync
        def _(sp):
            sp.dma_start(ident[:], dram["ident"]).then_inc(const_loaded, DMA)
            sp.dma_start(future[:], dram["future"]).then_inc(const_loaded, DMA)
            for p in range(2):
                for j in range(4):
                    sp.dma_start(Ks[0:ALIBI, p, :, j], dram["alibi_k"].rearrange("r (n t) -> r n t", t=TB)
                                 ).then_inc(const_loaded, DMA)
                    sp.dma_start(Ks[QK_ROWS:ROWS, p, :, j], dram["alibi_k"][2:4].rearrange("r (n t) -> r n t", t=TB)
                                 ).then_inc(const_loaded, DMA)
            for c in range(NT):
                load_q(sp, 0, c)
                load_k(sp, 0, 0, c)
                load_v(sp, 0, c)
            for c in range(NT):
                load_k(sp, 1, 1, c)

            def next_q(i, p, g):
                for c in range(NT):
                    sp.wait_ge(scores_ready, NTILE * i + 4 * first_step[NT * p + c + 1])
                    load_q(sp, g, c)

            def next_v(i, p, g):
                for c in range(NT):
                    n = first_step[NT * p + NT - 1] + SUB * (c + 1)
                    sp.wait_ge(pv_done, NSTEP * i + n + PSLOTS // 4)
                    load_v(sp, g, c)

            with sp.Fori(0, G // 2 - 1) as i:
                next_q(i, 0, 2 * i + 1)
                next_v(i, 0, 2 * i + 1)
                for c in range(NT):
                    load_k(sp, 2 * i + 2, 0, c)
                next_q(i, 1, 2 * i + 2)
                next_v(i, 1, 2 * i + 2)
                for c in range(NT):
                    load_k(sp, 2 * i + 3, 1, c)
            next_q(G // 2 - 1, 0, G - 1)
            next_v(G // 2 - 1, 0, G - 1)
            sp.wait_ge(chunk_stored, DMA * dram["ffn_w"].shape[0])
            sp.dma_start(w_early[:], dram["ffn_w_copy"][0:w_early.shape[1]].rearrange("n p f -> p n f")
                         ).then_inc(early_loaded, DMA)

        @block.tensor
        def _(pe):
            pe.sem_inc(pv_done, PSLOTS // 4)
            pe.wait_ge(const_loaded, CONST_DMAS * DMA)

            def ring_entry(i, r):
                kind, what = ring[r]
                pe.wait_ge(ring_free, NRING * i + r + 1)
                if kind == "turn":
                    pe.wait_ge(neg_ready, NTB * i + what + 1)
                    nc.tensor.transpose(max_psum[0:32, r % 2, 0:P // 2].bitcast(BF16),
                                        neg_parts[:, what % NT].rearrange("p c h u -> p (c h u)"), ident[:]
                                        ).then_inc(ring_ready, 1)
                    return
                if kind == "none":
                    nc.tensor.matmul(max_psum[:, r % 2, 0:P], ident[:], ident[:], start=True, stop=True
                                     ).then_inc(ring_ready, 1)
                    return
                p, tb, u, first, heads, c, blocks, _ = what
                if (u, first, c) == (0, 0, 0):
                    pe.wait_ge(q_loaded[tb], Q_DMAS * DMA * (2 * i + p + 1))
                    pe.wait_ge(k_loaded[p][tb], K_DMAS * DMA * (i + 1))
                for h in range(heads):
                    q_block = Qs[0:QK_ROWS, tb, first + h, u * P:(u + 1) * P]
                    for b in range(0, blocks, SUB):
                        w = min(SUB, blocks - b) * P
                        diag = 8 * c + b + w // P == SUB * tb + u + 1
                        at = h * (8 // heads) * P + b * P
                        mm = nc.tensor.matmul(max_psum[:, r % 2, at:at + w], q_block,
                                              Ks[0:QK_ROWS, p, (8 * c + b) // SUB, first + h, 0:w],
                                              start=True, stop=not diag)
                        if diag:
                            mm = nc.tensor.matmul(max_psum[:, r % 2, at + w - P:at + w], ident[:], future[:],
                                                  start=False, stop=True)
                mm.then_inc(ring_ready, 1)

            def score_tile(i, n, j):
                p, tb, s = steps[n]
                skip = max(0, s - SUB * tb) * P
                e = 4 * n + j
                out = score_psum[:, e % SLOTS, 0:TB - skip]
                diag = s >= SUB * tb
                pe.wait_ge(exp_done, NTILE * i + e + 1)
                mm = nc.tensor.matmul(out, Ks[0:ROWS, p, s // SUB, j, (s % SUB) * P:(s % SUB + 1) * P],
                                      Qs[0:ROWS, tb, j, skip:TB], start=True, stop=not diag)
                if diag:
                    mm = nc.tensor.matmul(out[:, 0:P], future[:], ident[:], start=False, stop=True)
                mm.then_inc(scores_ready, 1)

            def weigh(i, n):
                p, tb, s = steps[n]
                skip = max(0, s - SUB * tb) * P
                if s == 0:
                    pe.wait_ge(acc_copied, NTB * i + NT * p + tb + 1)
                if s == SUB * tb:
                    pe.wait_ge(v_loaded[tb], DMA * (2 * i + p + 1))
                pe.wait_ge(exp_done, NTILE * i + 4 * n + 4 + SLOTS)
                for j in range(4):
                    mm = nc.tensor.matmul(y_psum[32 * j:32 * j + 32, skip:TB], Vs[:, s, j, :],
                                          probs[:, (4 * n + j) % PSLOTS, 0:TB - skip],
                                          start=s == 0, stop=s == SUB * (tb + 1) - 1)
                mm.then_inc(pv_done, 1)

            with pe.Fori(0, G // 2) as i:
                for n in range(NSTEP):
                    p, tb, s = steps[n]
                    for j in range(4):
                        if s == 0 and j == 0:
                            if n == 0:
                                for r in ring_at[0]:
                                    ring_entry(i, r)
                            pe.wait_ge(max_loaded, 2 * DMA * (NTB * i + NT * p + tb + 1))
                        score_tile(i, n, j)
                        if j == 1 and n >= LAG:
                            weigh(i, n - LAG)
                        if n or j:
                            for r in ring_at[4 * n + j]:
                                ring_entry(i, r)
                for n in range(NSTEP - LAG, NSTEP):
                    weigh(i, n)

        @block.scalar
        def _(act):
            act.sem_inc(exp_done, SLOTS)
            act.sem_inc(acc_copied, 1)
            for b in range(2):
                act.sem_inc(y_stored[b], 1)
            y_dst = dram["yT"].rearrange("g p (n t) -> g n p t", t=TB)

            def store_y(i, k):
                act.wait_ge(y_ready, NTB * i + k + 3)
                act.dma_start(y_dst[2 * i + k // NT, k % NT], y_out[:, k % 2]).then_inc(y_stored[k % 2], DMA)

            def take_sums(i, k):
                act.wait_ge(pv_done, NSTEP * i + first_step[k + 1] + PSLOTS // 4)
                act.wait_ge(y_ready, NTB * i + k + 1)
                nc.scalar.activation(acc[:, k % 2], y_psum[:], ACT.Copy).then_inc(acc_copied, 1)
                if k >= 2:
                    store_y(i, k - 2)

            with act.Fori(0, G // 2) as i:
                for n in range(NSTEP):
                    p, tb, s = steps[n]
                    skip = max(0, s - SUB * tb) * P
                    act.wait_ge(pv_done, NSTEP * i + n + 1)
                    for j in range(4):
                        e = 4 * n + j
                        act.wait_ge(scores_ready, NTILE * i + e + 1)
                        nc.scalar.activation(probs[:, e % PSLOTS, 0:TB - skip], score_psum[:, e % SLOTS, 0:TB - skip],
                                             ACT.Exp).then_inc(exp_done, 1)
                        if s == LAG - 1 and n >= LAG and j == 2:
                            take_sums(i, NT * p + tb - 1)
                take_sums(i, NTB - 1)
                store_y(i, NTB - 2)
                store_y(i, NTB - 1)
            for b in range(2):
                act.wait_ge(y_stored[b], DMA * NT * (G // 2) + 1)

        @block.vector
        def _(dve):
            dve.sem_inc(ring_free, 2)

            def reduce_entry(i, r):
                kind, what = ring[r]
                dve.wait_ge(ring_ready, NRING * i + r + 1)
                if kind == "turn":
                    nc.vector.tensor_copy(neg_rows[:, what % NT], max_psum[0:32, r % 2, 0:P // 2].bitcast(BF16)
                                          ).then_inc(neg_rows_ready, 1)
                    dve.wait_ge(neg_rows_ready, NTB * i + what + 1)
                    dve.sem_inc(ring_free, 1)
                    return
                if kind == "none":
                    dve.sem_inc(ring_free, 1)
                    return
                p, tb, u, first, heads, c, blocks, last = what
                nc.vector.reduce_max(chunk_max[:, tb, first:first + heads, u, c],
                                     max_psum[:, r % 2].rearrange("p (h k) -> p h k", h=heads)[:, :, 0:blocks * P],
                                     AX_X).then_inc(ring_free, 1)
                if last:
                    small = 2 * (NTB * i + NT * p + tb)
                    dve.wait_ge(ring_free, NRING * i + r + 3)
                    nc.vector.reduce_max(row_max[:, tb], chunk_max[:, tb, :, :, 0:chunks[tb]], AX_X
                                         ).then_inc(small_done, 1)
                    dve.wait_ge(small_done, small + 1)
                    nc.vector.tensor_scalar_mul(neg_parts[:, tb, 0], row_max[:, tb], -1.0).then_inc(small_done, 1)
                    dve.wait_ge(small_done, small + 2)
                    nc.vector.scalar_tensor_tensor(out=neg_parts[:, tb, 1], in0=row_max[:, tb], scalar=-1.0,
                                                   in1=neg_parts[:, tb, 0], op0=ALU.mult, op1=ALU.subtract
                                                   ).then_inc(neg_ready, 1)

            def norm(i, k):
                dve.wait_ge(acc_copied, NTB * i + k + 2)
                nc.vector.reciprocal(recip[:, k % 2], acc[:, k % 2]).then_inc(norm_step, 1)
                dve.wait_ge(norm_step, NTB * i + k + 1)
                dve.sem_inc(waits_passed, 1)
                nc.vector.stream_shuffle(recip_y[:, k % 2], recip[:, k % 2],
                                         [D + r % D for r in range(32)]).then_inc(norm_ready, 1)

            def see_chunk(i, n):
                at = CHUNKS * i + n
                dve.wait_ge(chunk_loaded, DMA * at + DMA)
                dve.wait_ge(seen_step, at + 1)
                nc.vector.tensor_tensor(seen_bits[:], seen_bits[:], w_stage[:].bitcast(I32), ALU.bitwise_or
                                        ).then_inc(seen_step, 1)

            nc.vector.memset(seen_bits[:], 0).then_inc(seen_step, 1)
            with dve.Fori(0, G // 2) as i:
                for n in range(NSTEP):
                    p, tb, s = steps[n]
                    for j in range(4):
                        for r in ring_at[4 * n + j]:
                            reduce_entry(i, r)
                    if s == LAG and n >= 4:
                        norm(i, NT * p + tb - 1)
                    if s == 6 and NT * p + tb in quiet:
                        see_chunk(i, quiet.index(NT * p + tb))
                norm(i, NTB - 1)

        @block.gpsimd
        def _(pool):
            pool.sem_inc(y_ready, 2)

            def send_max(i, k):
                pool.wait_ge(neg_rows_ready, NTB * i + k + 1)
                pool.sem_inc(waits_passed, 1)
                for part in range(2):
                    pool.dma_start(Qs[QK_ROWS + part:QK_ROWS + part + 1, k % NT].rearrange("p j t -> p (j t)"),
                                   neg_rows[16 * part:16 * part + 16, k % NT]).then_inc(max_loaded, DMA)

            def scale_y(i, k):
                pool.wait_ge(norm_ready, NTB * i + k + 1)
                pool.wait_ge(y_stored[k % 2], DMA * (NT * i + k // 2) + 1)
                nc.gpsimd.tensor_tensor(y_out[:, k % 2], acc[:, k % 2], recip_y[:, k % 2], ALU.mult
                                        ).then_inc(y_ready, 1)

            def see_chunk(i, n):
                at = CHUNKS * i + n
                pool.dma_start(w_stage[:], dram["ffn_w"][at]).then_inc(chunk_loaded, DMA)
                pool.wait_ge(chunk_loaded, DMA * at + DMA)
                pool.sem_inc(waits_passed, 1)
                pool.dma_start(dram["ffn_w_copy"][at], w_stage[:]).then_inc(chunk_stored, DMA)
                pool.wait_ge(seen_step, at + 2)
                pool.wait_ge(chunk_stored, DMA * at + DMA)
                pool.sem_inc(waits_passed, 1)

            with pool.Fori(0, G // 2) as i:
                send_max(i, 0)
                for k in range(1, NTB):
                    send_max(i, k)
                    scale_y(i, k - 1)
                    if k in quiet:
                        see_chunk(i, quiet.index(k))
                scale_y(i, NTB - 1)


def ffn(nc, dram, T, C, H, F, seen_bits, w_early, early_loaded):
    NT = T // TB
    SUB = TB // P
    BANKS = SUB // 2
    KC = C // P
    KF = F // P
    G = H // 4
    D = C // H
    SPLITS = 3 * KF
    HT = 4 * KF
    RING = 4
    assert 2 * C == TB and KF > RING

    with ExitStack() as ctx:
        def sb(name, shape, dt):
            return ctx.enter_context(nc.sbuf_tensor(name, shape, dt))

        def ps(name, shape, dt):
            return ctx.enter_context(nc.psum_tensor(name, shape, dt))

        def sem(name):
            return ctx.enter_context(nc.semaphore(name))

        w_late = sb("w_late", [P, 2 * KF, F], F32)
        w1, w2 = w_early[:, 0:KC], w_early[:, KC:2 * KC]
        w5 = w_early[:, 2 * KC:3 * KC].rearrange("p a (b n) -> p (a b) n", n=C)
        w3, w4 = w_late[:, 0:KF], w_late[:, KF:2 * KF]
        w_proj = sb("w_proj", [P, KC, C], F32)
        b_proj = sb("b_proj", [P, 2, C], F32)
        scales = sb("scales", [P, 4, KF], F32)
        s5 = sb("s5", [P, 2, C], F32)
        ident = sb("ident_f", [P, P], F32)
        minus_half = sb("minus_half", [P, SUB], F32)
        ones = sb("ones", [P, 1], F32)
        low_bits = sb("low_bits", [P, 1], I32)
        low_bits_f = sb("low_bits_f", [P, 1], F32)
        low_sum = sb("low_sum", [1, 1], I32)
        yT = sb("yT", [P, KC, TB], F32)
        x = sb("x", [P, SUB, C], F32)
        z = sb("z", [P, SUB, C], F32)
        x1 = sb("x1", [P, SUB, C], F32)
        x1_kept = sb("x1_kept", [P, SUB, C], F32)
        out_sb = sb("out_sb", [P, SUB, C], F32)
        x1T_hi = sb("x1T_hi", [P, KC, TB], F32R)
        x1T_lo = sb("x1T_lo", [P, KC, TB], F32R)
        gate = sb("gate", [P, 2, TB], F32)
        full = sb("full_f", [P, RING, TB], F32)
        hid_hi = sb("hid_hi", [P, 2, KF, TB], F32R)
        hid_lo = sb("hid_lo", [P, 2, KF, TB], F32R)
        stats = sb("stats", [P, SUB, 6], F32)
        moments = sb("moments", [P, SUB, 2], F32)
        var_eps = sb("var_eps", [P, SUB], F32)
        rstd = sb("rstd", [P, SUB], F32)
        row_psum = ps("row_psum", [P, BANKS, 2, C], F32)
        turn_psum = ps("turn_psum", [P, KC, TB], F32)
        hid_psum = ps("hid_psum", [P, RING, TB], F32)

        consts_loaded = sem("consts_loaded_f")
        w3_loaded = sem("w3_loaded")
        w4_loaded = sem("w4_loaded")
        low_step = sem("low_step")
        low_summed = sem("low_summed")
        branch_ready = sem("branch_ready")
        y_loaded = sem("y_loaded")
        x_loaded = sem("x_loaded_f")
        proj_ready = sem("proj_ready")
        z_ready = sem("z_ready")
        stat_step = sem("stat_step")
        var_ready = sem("var_ready")
        rstd_ready = sem("rstd_ready")
        x1_ready = sem("x1_ready")
        kept_ready = sem("kept_ready")
        kept_used = sem("kept_used")
        turned = sem("turned")
        x1T_hi_ready = sem("x1T_hi_ready")
        x1T_ready = sem("x1T_ready")
        hid_ready = sem("hid_ready")
        gate_ready = sem("gate_ready")
        gated = sem("gated")
        hi_ready = sem("hi_ready")
        lo_ready = sem("lo_ready")
        down_ready = sem("down_ready")
        z2_ready = sem("z2_ready")
        sum_step = sem("sum_step")
        out_ready = sem("out_ready")
        out_stored = sem("out_stored")
        waits_passed = sem("waits_passed")
        block = ctx.enter_context(nc.Block())

        @block.sync
        def _(sp):
            sp.sem_inc(out_stored, 1)
            y_src = dram["yT"].rearrange("g (j e) (n t) -> n g j e t", j=4, t=TB)
            x_src = dram["x"].rearrange("(n s p) c -> n p s c", s=SUB, p=P)
            dst = dram["out"].rearrange("(n s p) c -> n p s c", s=SUB, p=P)
            JD = 4 * D

            def load(t, first):
                if not first:
                    sp.wait_ge(proj_ready, BANKS * t)
                for g in range(G):
                    at = JD * g % P
                    sp.dma_start(yT[at:at + JD, JD * g // P], y_src[t, g, :, 0:D]).then_inc(y_loaded, DMA)
                if not first:
                    sp.wait_ge(z_ready, BANKS * t + 1)
                sp.dma_start(x[:], x_src[t]).then_inc(x_loaded, DMA)

            def store(t):
                sp.wait_ge(out_ready, SUB * t + SUB)
                sp.dma_start(dst[t], out_sb[:]).then_inc(out_stored, DMA)

            sp.dma_start(w_proj[:], dram["w_proj"].rearrange("(k p) n -> p k n", p=P)).then_inc(consts_loaded, DMA)
            load(0, True)
            sp.dma_start(b_proj[:], dram["b_proj"].rearrange("p (a c) -> p a c", a=2)).then_inc(consts_loaded, DMA)
            sp.dma_start(s5[:], dram["s5"].rearrange("p (a c) -> p a c", a=2)).then_inc(consts_loaded, DMA)
            sp.dma_start(ident[:], dram["ident_f"]).then_inc(consts_loaded, DMA)
            sp.dma_start(scales[:], dram["scales"]).then_inc(consts_loaded, DMA)
            for lay, loaded in enumerate((w3_loaded, w4_loaded)):
                for k in range(KF):
                    sp.dma_start(w_late[:, KF * lay + k], dram["ffn_w_copy"][3 * KC + KF * lay + k]).then_inc(loaded, DMA)
            load(1, False)
            with sp.Fori(1, NT - 1) as i:
                load(i + 1, False)
                store(i - 1)
            store(NT - 2)
            store(NT - 1)
            sp.wait_ge(out_stored, DMA * NT + 1)

        @block.gpsimd
        def _(pool):
            pool.wait_ge(early_loaded, DMA)
            nc.gpsimd.memset(minus_half[:], -0.5).then_inc(rstd_ready, 1)
            pool.wait_ge(rstd_ready, 1)

            def power(n):
                pool.wait_ge(var_ready, n + 1)
                nc.gpsimd.tensor_tensor(rstd[:], var_eps[:], minus_half[:], ALU.pow).then_inc(rstd_ready, 1)

            def keep(i):
                pool.wait_ge(x1_ready, SUB * i + SUB)
                pool.wait_ge(kept_used, i + 1)
                pool.sem_inc(waits_passed, 1)
                nc.gpsimd.tensor_copy(x1_kept[:], x1[:]).then_inc(kept_ready, 1)

            power(0)
            keep(0)
            power(1)
            with pool.Fori(1, NT - 1) as i:
                power(2 * i)
                keep(i)
                power(2 * i + 1)
            power(2 * NT - 2)
            keep(NT - 1)
            power(2 * NT - 1)

        @block.tensor
        def _(pe):
            def project_out(t, first):
                pe.wait_ge(y_loaded, DMA * G * t + DMA * G)
                if not first:
                    pe.wait_ge(z2_ready, BANKS * t - BANKS + 1)
                for s in range(SUB):
                    for k in range(KC):
                        mm = nc.tensor.matmul(row_psum[:, s // 2, s % 2], yT[:, k, s * P:(s + 1) * P], w_proj[:, k],
                                              start=k == 0, stop=k == KC - 1)
                    if s % 2:
                        mm.then_inc(proj_ready, 1)

            def transpose(t):
                for s in range(SUB):
                    pe.wait_ge(x1_ready, SUB * t + s + 1)
                    for k in range(KC):
                        mm = nc.tensor.transpose(turn_psum[:, k, s * P:(s + 1) * P], x1[:, s, k * P:(k + 1) * P], ident[:])
                mm.then_inc(turned, 1)

            def layers(i, last, exact):
                def weights(ap):
                    return ap.bitcast(F32R) if exact else ap

                def parts(hi, lo):
                    return enumerate((hi, lo) if exact else (hi.bitcast(F32), lo.bitcast(F32)))

                pe.wait_ge(x1T_ready, KC * i + KC)
                for m in range(KF):
                    if m >= 2:
                        pe.wait_ge(gated, KF * i + m + 1)
                    for t, w in enumerate((w1, w2)):
                        for k in range(KC):
                            for c, part in parts(x1T_hi[:, k], x1T_lo[:, k]):
                                mm = nc.tensor.matmul(hid_psum[:, (2 * m + t) % RING], weights(w[:, k, m * P:(m + 1) * P]),
                                                      part, start=(k, c) == (0, 0), stop=(k, c) == (KC - 1, 1))
                        mm.then_inc(hid_ready, 1)
                for lay, (w, loaded) in enumerate(((w3, w3_loaded), (w4, w4_loaded))):
                    pe.wait_ge(loaded, DMA * KF)
                    for m in range(KF):
                        before = SPLITS * i + KF * lay + m
                        if lay == 0 and m == 0:
                            pe.wait_ge(gated, KF * i + KF + 1)
                        elif lay == 1 or m >= RING:
                            pe.wait_ge(hi_ready, before + KF - RING + 1)
                        for k in range(KF):
                            if m == 0:
                                pe.wait_ge(lo_ready, before + k + 1 + RING)
                            for c, part in parts(hid_hi[:, lay, k], hid_lo[:, lay, k]):
                                mm = nc.tensor.matmul(hid_psum[:, m % RING], weights(w[:, k, m * P:(m + 1) * P]),
                                                      part, start=(k, c) == (0, 0), stop=(k, c) == (KF - 1, 1))
                        mm.then_inc(hid_ready, 1)
                        if not last and (lay, m) == PROJECT_AFTER:
                            project_out(i + 1, False)
                        if not last and (lay, m) == TRANSPOSE_AFTER:
                            transpose(i + 1)
                if not last:
                    pe.wait_ge(z_ready, BANKS * i + 2 * BANKS + 1)
                else:
                    pe.wait_ge(z2_ready, BANKS * i + 1)
                for s in range(SUB):
                    for k in range(KF):
                        if s == 0:
                            pe.wait_ge(lo_ready, SPLITS * i + 2 * KF + k + 1 + RING)
                        for c, part in parts(hid_hi[:, 0, k, s * P:(s + 1) * P], hid_lo[:, 0, k, s * P:(s + 1) * P]):
                            mm = nc.tensor.matmul(row_psum[:, s // 2, s % 2], part, weights(w5[:, k]),
                                                  start=(k, c) == (0, 0), stop=(k, c) == (KF - 1, 1))
                    if s % 2:
                        mm.then_inc(down_ready, 1)

            pe.wait_ge(consts_loaded, 5 * DMA)
            project_out(0, True)
            pe.wait_ge(low_step, 4)
            nc.tensor.matmul(turn_psum[0:1, 0, 0:1], low_bits_f[:], ones[:], start=True, stop=True).then_inc(low_summed, 1)
            pe.wait_ge(branch_ready, 1)
            transpose(0)
            pe.wait_ge(early_loaded, DMA)
            beyond = pe.value_load(low_sum[0:1, 0:1])
            with pe.If(beyond == 0):
                with pe.Fori(0, NT - 1) as i:
                    layers(i, False, True)
                layers(NT - 1, True, True)
            with pe.Else():
                with pe.Fori(0, NT - 1) as i:
                    layers(i, False, False)
                layers(NT - 1, True, False)

        @block.scalar
        def _(act):
            act.wait_ge(consts_loaded, 5 * DMA)

            def split_x1T(t):
                act.wait_ge(turned, t + 1)
                for k in range(KC):
                    nc.scalar.activation(x1T_hi[:, k], turn_psum[:, k], ACT.Copy).then_inc(x1T_hi_ready, 1)

            def layers(i, last):
                def gate_hi(m):
                    act.wait_ge(gated, KF * i + m + 3)
                    nc.scalar.activation(hid_hi[:, 0, m], full[:, m % RING], ACT.Copy).then_inc(hi_ready, 1)

                for m in range(KF):
                    act.wait_ge(hid_ready, HT * i + 2 * m + 1)
                    act.wait_ge(gated, KF * i + m + 1)
                    nc.scalar.activation(gate[:, m % 2], hid_psum[:, (2 * m) % RING], ACT.Silu,
                                         scale=scales[:, 0, m:m + 1]).then_inc(gate_ready, 1)
                    if m >= 1:
                        gate_hi(m - 1)
                gate_hi(KF - 1)
                for lay in range(2):
                    for m in range(KF):
                        n = KF * (1 + lay) + m
                        act.wait_ge(hid_ready, HT * i + KF + n + 1)
                        act.wait_ge(lo_ready, SPLITS * i + n + 1)
                        nc.scalar.activation(full[:, m % RING], hid_psum[:, m % RING], ACT.Gelu,
                                             scale=scales[:, 2 + lay, m:m + 1])
                        nc.scalar.activation(hid_hi[:, 1 - lay, m], hid_psum[:, m % RING], ACT.Gelu,
                                             scale=scales[:, 2 + lay, m:m + 1]).then_inc(hi_ready, 1)
                        if not last and (lay, m) == TRANSPOSE_AFTER:
                            split_x1T(i + 1)

            split_x1T(0)
            with act.Fori(0, NT - 1) as i:
                layers(i, False)
            layers(NT - 1, True)

        @block.vector
        def _(dve):
            dve.sem_inc(z_ready, 1)
            dve.sem_inc(z2_ready, 1)
            dve.sem_inc(kept_used, 1)
            dve.sem_inc(gated, 2)
            dve.sem_inc(lo_ready, RING)

            nc.vector.memset(ones[:], 1.0).then_inc(low_step, 1)
            nc.vector.tensor_scalar(seen_bits[:], seen_bits[:], BEYOND_F32R, None, ALU.bitwise_and).then_inc(low_step, 1)
            dve.wait_ge(low_step, 2)
            nc.vector.reduce_max(low_bits[:], seen_bits[:], AX_X).then_inc(low_step, 1)
            dve.wait_ge(low_step, 3)
            nc.vector.tensor_copy(low_bits_f[:], low_bits[:]).then_inc(low_step, 1)
            dve.wait_ge(low_summed, 1)
            nc.vector.tensor_copy(low_sum[:], turn_psum[0:1, 0, 0:1]).then_inc(branch_ready, 1)
            dve.wait_ge(consts_loaded, 5 * DMA)

            def moments_of(n, src):
                for s in range(SUB):
                    nc.vector.bn_stats(stats[:, s], src[:, s]).then_inc(stat_step, 1)
                dve.wait_ge(stat_step, 2 * SUB * n + SUB)
                dve.sem_inc(waits_passed, 1)
                for s in range(SUB):
                    nc.vector.bn_aggr(moments[:, s], stats[:, s]).then_inc(stat_step, 1)
                dve.wait_ge(stat_step, 2 * SUB * n + 2 * SUB)
                nc.vector.tensor_scalar_add(var_eps[:], moments[:, :, 1], EPS).then_inc(var_ready, 1)

            def normalise(n, src, dst, ready):
                dve.wait_ge(rstd_ready, n + 2)
                for s in range(SUB):
                    nc.vector.tensor_scalar(dst[:, s], src[:, s], moments[:, s, 0:1], rstd[:, s:s + 1],
                                            ALU.subtract, ALU.mult).then_inc(ready, 1)

            def first_sum(t, n):
                dve.wait_ge(x_loaded, DMA * t + DMA)
                for b in range(BANKS):
                    add = nc.vector.tensor_add(z[:, 2 * b:2 * b + 2], x[:, 2 * b:2 * b + 2], b_proj[:])
                add.then_inc(sum_step, 1)
                dve.wait_ge(sum_step, t + 1)
                for b in range(BANKS):
                    dve.wait_ge(proj_ready, BANKS * t + b + 1)
                    nc.vector.tensor_add(z[:, 2 * b:2 * b + 2], z[:, 2 * b:2 * b + 2], row_psum[:, b]).then_inc(z_ready, 1)
                dve.wait_ge(z_ready, BANKS * t + BANKS + 1)
                moments_of(n, z)

            def second_sum(t, n):
                for b in range(BANKS):
                    dve.wait_ge(down_ready, BANKS * t + b + 1)
                    nc.vector.tensor_mul(z[:, 2 * b:2 * b + 2], row_psum[:, b], s5[:]).then_inc(z2_ready, 1)
                dve.wait_ge(z2_ready, BANKS * t + BANKS + 1)
                dve.wait_ge(kept_ready, t + 1)
                nc.vector.tensor_add(z[:], z[:], x1_kept[:]).then_inc(kept_used, 1)
                dve.wait_ge(kept_used, t + 2)
                moments_of(n, z)

            def normalise_out(t, n):
                dve.wait_ge(out_stored, DMA * t + 1)
                normalise(n, z, out_sb, out_ready)

            def split_x1T(t):
                for k in range(KC):
                    dve.wait_ge(x1T_hi_ready, KC * t + k + 1)
                    nc.vector.tensor_sub(x1T_lo[:, k], turn_psum[:, k], x1T_hi[:, k].bitcast(F32)).then_inc(x1T_ready, 1)

            def layers(i, first, last):
                def split(n):
                    lay, m = n // KF, n % KF
                    dve.wait_ge(hi_ready, SPLITS * i + n + 1)
                    nc.vector.tensor_sub(hid_lo[:, lay % 2, m], full[:, m % RING], hid_hi[:, lay % 2, m].bitcast(F32)
                                         ).then_inc(lo_ready, 1)

                for m in range(KF):
                    dve.wait_ge(gate_ready, KF * i + m + 1)
                    dve.wait_ge(hid_ready, HT * i + 2 * m + 2)
                    dve.wait_ge(lo_ready, SPLITS * i + m + 1)
                    nc.vector.scalar_tensor_tensor(out=full[:, m % RING], in0=hid_psum[:, (2 * m + 1) % RING],
                                                   scalar=scales[:, 1, m:m + 1], in1=gate[:, m % 2],
                                                   op0=ALU.mult, op1=ALU.mult).then_inc(gated, 1)
                    if m >= 1:
                        split(m - 1)
                split(KF - 1)
                if not first:
                    dve.wait_ge(x1_ready, SUB * i + SUB)
                    second_sum(i - 1, 2 * i)
                split(KF)
                split(KF + 1)
                if not first:
                    normalise_out(i - 1, 2 * i)
                for m in range(2, KF):
                    split(KF + m)
                    if not last and (0, m) == PROJECT_AFTER:
                        if not first:
                            dve.wait_ge(out_ready, SUB * i)
                        first_sum(i + 1, 2 * i + 1)
                    if not last and (0, m - 1) == PROJECT_AFTER:
                        dve.wait_ge(kept_ready, i + 1)
                        normalise(2 * i + 1, z, x1, x1_ready)
                for m in range(KF):
                    split(2 * KF + m)
                    if not last and (1, m) == TRANSPOSE_AFTER:
                        split_x1T(i + 1)

            first_sum(0, 0)
            normalise(0, z, x1, x1_ready)
            split_x1T(0)
            layers(0, True, False)
            with dve.Fori(1, NT - 1) as i:
                layers(i, False, False)
            layers(NT - 1, False, True)
            dve.wait_ge(x1_ready, SUB * NT)
            second_sum(NT - 1, 2 * NT - 1)
            normalise_out(NT - 1, 2 * NT - 1)


def build(nc, dram, T, C, H, F):
    with ExitStack() as ctx:
        seen_bits = ctx.enter_context(nc.sbuf_tensor("seen_bits", [P, F], I32))
        w_early = ctx.enter_context(nc.sbuf_tensor("w_early", [P, 3 * (C // P), F], F32))
        early_loaded = ctx.enter_context(nc.semaphore("early_loaded"))
        project(nc, dram, T, C, H)
        attention(nc, dram, T, C, H, F, seen_bits, w_early, early_loaded)
        ffn(nc, dram, T, C, H, F, seen_bits, w_early, early_loaded)


def kernel(**inputs):
    import numpy as np
    import concourse.bacc as bacc
    from concourse import mybir as _mybir
    from concourse.bass_utils import run_bass_kernel_spmd

    x = np.ascontiguousarray(inputs["L0_attn_x"])[0]
    T, C = x.shape
    H = 16
    F = inputs["L0_ffn_w1_w"].shape[0]
    w_attn = np.ascontiguousarray(inputs["L0_attn_W_attn"])
    b_attn = np.ascontiguousarray(inputs["L0_attn_b_attn"])

    def bf16_bits(a):
        return (np.ascontiguousarray(a, dtype=np.float32).view(np.uint32) >> 16).astype(np.uint16)

    def rows(v):
        return np.ascontiguousarray(np.broadcast_to(v, (128, v.shape[0])))

    def columns(v):
        return np.ascontiguousarray(np.asarray(v).reshape(-1, 128).T)

    def chunks(w):
        blocks = np.asarray(w).T.reshape(-1, 128, w.shape[0]).transpose(1, 0, 2)
        return blocks.reshape(128, -1, F).transpose(1, 0, 2)

    pos = np.arange(T)
    slope = 0.5 ** np.arange(1, H + 1)[:, None]
    alibi_k = np.stack([pos % 128, pos - pos % 128, np.ones(T), np.ones(T)])
    alibi_q = np.stack([slope + 0 * pos, slope + 0 * pos, -slope * (pos % 128), -slope * (pos - pos % 128)], axis=1)
    future = np.where(np.arange(128)[None, :] > np.arange(128)[:, None], -1e30, 0.0)
    arrays = {
        "x": x,
        "xT": np.ascontiguousarray(x.T),
        "w_attn": w_attn,
        "b_qk": columns(b_attn[:2 * C]),
        "b_v": rows(b_attn[2 * C:]),
        "w_proj": np.ascontiguousarray(inputs["L0_attn_W_proj"]),
        "b_proj": rows(np.tile(np.asarray(inputs["L0_attn_b_proj"]), 2)),
        "ffn_w": np.concatenate([chunks(inputs[f"L0_ffn_{n}_w"]) for n in ("w1", "w2", "w3", "h1", "h2")]),
        "scales": np.ascontiguousarray(np.stack([columns(inputs[f"L0_ffn_{n}_s"]) for n in ("w1", "w2", "h1", "h2")], 1)),
        "s5": rows(np.tile(np.asarray(inputs["L0_ffn_w3_s"]), 2)),
        "ident_f": np.eye(128, dtype=np.float32),
        "ident": bf16_bits(np.eye(128)),
        "future": bf16_bits(future),
        "alibi_k": bf16_bits(alibi_k),
        "alibi_q": bf16_bits(alibi_q),
    }
    nc = bacc.Bacc("TRN2", target_bir_lowering=False, num_devices=1)
    dram = {}
    for name, a in arrays.items():
        ap = nc.dram_tensor(name + "_dram", a.shape, _mybir.dt.from_np(a.dtype), kind="ExternalInput").ap()
        dram[name] = ap.bitcast(_mybir.dt.bfloat16) if a.dtype == np.uint16 else ap
    dram["parts"] = nc.dram_tensor("parts_dram", (3, 2 * C, T), _mybir.dt.bfloat16, kind="Internal").ap()
    dram["v_ones"] = nc.dram_tensor("v_ones_dram", (H // 4, 128, T // 128, 128), _mybir.dt.float32, kind="Internal").ap()
    dram["yT"] = nc.dram_tensor("yT_dram", (H // 4, 128, T), _mybir.dt.float32, kind="Internal").ap()
    dram["ffn_w_copy"] = nc.dram_tensor("ffn_w_copy_dram", arrays["ffn_w"].shape, _mybir.dt.float32, kind="Internal").ap()
    dram["out"] = nc.dram_tensor("out_dram", (T, C), _mybir.dt.float32, kind="ExternalOutput").ap()
    build(nc, dram, T, C, H, F)
    r = run_bass_kernel_spmd(nc, [{k + "_dram": v for k, v in arrays.items()}], core_ids=[0])
    return r.results[0]["out_dram"].reshape(1, T, C)
```

```python
from contextlib import ExitStack

import concourse.bass as bass
from concourse import mybir

ALU = mybir.AluOpType
ACT = mybir.ActivationFunctionType
F32 = mybir.dt.float32
F32R = mybir.dt.float32r
I32 = mybir.dt.int32
BF16 = mybir.dt.bfloat16
U16 = mybir.dt.uint16
AX_X = mybir.AxisListType.X

P = 128
TB = 512
DMA = 16
EPS = 1e-5

Q_PART = (0, 0, 1, 0, 2, 1)
K_PART = (0, 1, 0, 2, 0, 1)
ALIBI = 4
HEAD = 16

PROJECT_AFTER = (0, 6)
TRANSPOSE_AFTER = (1, 2)
BEYOND_F32R = 0xFFF


def load_constants(sp, dram, shared, Q_ROWS):
    sp.dma_start(shared.ident[:], dram["ident"]).then_inc(shared.const_loaded, DMA)
    sp.dma_start(shared.future[:], dram["future"]).then_inc(shared.const_loaded, DMA)
    rows = dram["alibi_k"].rearrange("r (n t) -> r n t", t=TB)
    for p in range(2):
        for j in range(4):
            sp.dma_start(shared.Ks[0:ALIBI, p, :, j], rows).then_inc(shared.const_loaded, DMA)
            sp.dma_start(shared.Ks[Q_ROWS:Q_ROWS + 2, p, :, j], rows[2:4]).then_inc(shared.const_loaded, DMA)


CONST_DMAS = 2 + 2 * 4 * 2


def project(nc, dram, T, C, H, shared):
    NT = T // TB
    KC = C // P
    MQK = 2 * C // P
    SUB = TB // P
    D = C // H
    G = H // 4
    SCALE = float(D) ** -0.5
    assert NT % 2 == 0 and D == HEAD and 2 * D == 32

    with ExitStack() as ctx:
        def sb(name, shape, dt):
            return ctx.enter_context(nc.sbuf_tensor(name, shape, dt))

        def sem(name):
            return ctx.enter_context(nc.semaphore(name))

        xT = sb("xT", [P, 2, KC, TB], F32)
        w_qkv = sb("w_qkv", [P, KC, 3 * C], F32)
        b_qk = sb("b_qk", [P, MQK], F32)
        b_qk_scaled = sb("b_qk_scaled", [P, MQK], F32)
        b_v = sb("b_v", [P, C], F32)
        full = sb("full", [P, 2, TB], F32)
        rest = sb("rest", [P, 2, TB], F32)
        parts = sb("parts", [P, 4, 3, TB], BF16)
        v_ones = sb("v_ones", [P, 2, SUB, G, 4, 2, D], F32)
        qk_psum = ctx.enter_context(nc.psum_tensor("qk_psum", [P, MQK, TB], F32))
        v_psum = ctx.enter_context(nc.psum_tensor("v_psum", [P, SUB // 2, 2, C], F32))

        w_loaded = sem("w_loaded")
        x_loaded = [sem("x_loaded_0"), sem("x_loaded_1")]
        bias_ready = sem("bias_ready")
        ones_ready = sem("ones_ready")
        qk_ready = sem("qk_ready")
        v_ready = sem("v_ready")
        full_ready = sem("full_ready")
        step_done = sem("step_done")
        parts_ready = sem("parts_ready")
        parts_stored = [sem(f"parts_stored_{i}") for i in range(4)]
        v_sb_ready = sem("v_sb_ready")
        v_stored = [sem("v_stored_0"), sem("v_stored_1")]
        waits_passed = sem("waits_passed")
        block = ctx.enter_context(nc.Block())

        @block.sync
        def _(sp):
            sp.dma_start(w_qkv[:], dram["w_attn"].rearrange("(k p) n -> p k n", p=P)).then_inc(w_loaded, DMA)
            sp.dma_start(b_qk[:], dram["b_qk"]).then_inc(w_loaded, DMA)
            sp.dma_start(b_v[:], dram["b_v"]).then_inc(w_loaded, DMA)
            for stored in (*parts_stored, *v_stored):
                sp.sem_inc(stored, 1)
            load_constants(sp, dram, shared, ALIBI + len(Q_PART) * D)
            part_dst = dram["parts"].rearrange("c (m p) (n t) -> n m p c t", p=P, t=TB)
            v_dst = dram["v_ones"].rearrange("g p (n s) e -> n g p s e", s=SUB)
            with sp.Fori(0, NT // 2) as i:
                for u in range(2):
                    for m in range(MQK):
                        sp.wait_ge(parts_ready, 2 * MQK * i + MQK * u + m + 3)
                        sp.sem_inc(waits_passed, 1)
                        sp.dma_start(part_dst[2 * i + u, m], parts[:, m]).then_inc(parts_stored[m], DMA)
                    sp.wait_ge(v_sb_ready, 2 * i + u + 2)
                    sp.sem_inc(waits_passed, 1)
                    for g in range(G):
                        sp.dma_start(v_dst[2 * i + u, g],
                                     v_ones[:, u, :, g].rearrange("p s j c d -> p s (j c d)")
                                     ).then_inc(v_stored[u], DMA)
            for m in range(MQK):
                sp.wait_ge(parts_stored[m], DMA * NT + 1)
            for u in range(2):
                sp.wait_ge(v_stored[u], DMA * G * NT // 2 + 1)

        @block.tensor
        def _(pe):
            pe.sem_inc(v_ready, 2)
            pe.wait_ge(w_loaded, 3 * DMA)
            with pe.Fori(0, NT // 2) as i:
                for u in range(2):
                    pe.wait_ge(x_loaded[u], DMA * i + DMA)
                    for m in range(MQK):
                        pe.wait_ge(full_ready, 2 * MQK * i + MQK * u + m + 1)
                        for k in range(KC):
                            mm = nc.tensor.matmul(qk_psum[:, m, :], w_qkv[:, k, m * P:(m + 1) * P],
                                                  xT[:, u, k, :], start=k == 0, stop=k == KC - 1)
                        mm.then_inc(qk_ready, 1)
                    pe.wait_ge(v_sb_ready, 2 * i + u + 1)
                    for s in range(SUB):
                        for k in range(KC):
                            mm = nc.tensor.matmul(v_psum[:, s // 2, s % 2, :], xT[:, u, k, s * P:(s + 1) * P],
                                                  w_qkv[:, k, 2 * C:3 * C], start=k == 0, stop=k == KC - 1)
                    mm.then_inc(v_ready, 1)

        @block.scalar
        def _(act):
            act.sem_inc(full_ready, MQK)
            act.wait_ge(bias_ready, 1)
            with act.Fori(0, NT // 2) as i:
                for u in range(2):
                    for m in range(MQK):
                        n = MQK * u + m
                        scale = SCALE if m < MQK // 2 else 1.0
                        act.wait_ge(qk_ready, 2 * MQK * i + n + 1)
                        act.wait_ge(parts_ready, 2 * MQK * i + n + 1)
                        act.wait_ge(parts_stored[m], 2 * DMA * i + DMA * u + 1)
                        nc.scalar.activation(full[:, m % 2], qk_psum[:, m, :], ACT.Identity,
                                             bias=b_qk_scaled[:, m:m + 1], scale=scale)
                        nc.scalar.activation(parts[:, m, 0], qk_psum[:, m, :], ACT.Identity,
                                             bias=b_qk_scaled[:, m:m + 1], scale=scale).then_inc(full_ready, 1)

        @block.vector
        def _(dve):
            dve.sem_inc(parts_ready, 2)
            dve.sem_inc(v_sb_ready, 1)
            nc.vector.memset(v_ones[:], 1.0).then_inc(ones_ready, 1)
            dve.wait_ge(w_loaded, 3 * DMA)
            h = MQK // 2
            nc.vector.tensor_scalar_mul(b_qk_scaled[:, 0:h], b_qk[:, 0:h], SCALE)
            nc.vector.tensor_copy(b_qk_scaled[:, h:MQK], b_qk[:, h:MQK]).then_inc(bias_ready, 1)
            dve.wait_ge(ones_ready, 1)
            with dve.Fori(0, NT // 2) as i:
                for u in range(2):
                    for m in range(MQK):
                        n = MQK * u + m
                        dve.wait_ge(full_ready, 2 * MQK * i + n + 1 + MQK)
                        nc.vector.tensor_sub(rest[:, m % 2], full[:, m % 2], parts[:, m, 0]).then_inc(step_done, 1)
                        dve.wait_ge(step_done, 4 * MQK * i + 2 * n + 1)
                        nc.vector.tensor_copy(parts[:, m, 1], rest[:, m % 2]).then_inc(step_done, 1)
                        dve.wait_ge(step_done, 4 * MQK * i + 2 * n + 2)
                        nc.vector.tensor_sub(parts[:, m, 2], rest[:, m % 2], parts[:, m, 1]).then_inc(parts_ready, 1)
                    dve.wait_ge(v_ready, 2 * i + u + 3)
                    dve.wait_ge(v_stored[u], DMA * G * i + 1)
                    for s in range(SUB):
                        add = nc.vector.tensor_add(
                            v_ones[:, u, s, :, :, 0, :].rearrange("p g j d -> p (g j) d"),
                            v_psum[:, s // 2, s % 2, :].rearrange("p (h d) -> p h d", d=D),
                            b_v[:].rearrange("p (h d) -> p h d", d=D))
                    add.then_inc(v_sb_ready, 1)

        @block.gpsimd
        def _(pool):
            x_src = dram["xT"].rearrange("(k p) (n t) -> n p k t", p=P, t=TB)
            with pool.Fori(0, NT // 2) as i:
                for u in range(2):
                    pool.wait_ge(v_ready, 2 * i + u + 1)
                    pool.sem_inc(waits_passed, 1)
                    pool.dma_start(xT[:, u], x_src[2 * i + u]).then_inc(x_loaded[u], DMA)


def plan(NT, SUB):
    LEAD = 3
    steps = [(p, tb, s) for p in range(2) for tb in range(NT) for s in range(SUB * (tb + 1))]
    first_step = [n for n, (_, _, s) in enumerate(steps) if s == 0] + [len(steps)]
    chunks = [-(-SUB * (tb + 1) // 8) for tb in range(NT)]
    ring, late = [], []
    for p in range(2):
        for tb in range(NT):
            for c in range(chunks[tb]):
                for u in range(SUB):
                    blocks = min(8, SUB * tb + u + 1 - 8 * c)
                    heads = 4 if blocks <= 2 else 2 if blocks <= 4 else 1
                    for j in range(0, 4, heads):
                        if late and late[0][0] == len(ring):
                            ring.append(("turn", late.pop(0)[1]))
                        last = (c, u, j + heads) == (chunks[tb] - 1, SUB - 1, 4)
                        ring.append(("unit", (p, tb, u, j, heads, c, blocks, last)))
            late.append((len(ring) + 3, NT * p + tb))
    ring.append(("turn", late.pop(0)[1]))

    work, time_of = [0.0], [0.0]
    for kind, what in ring:
        work.append(work[-1] + (65 + 133 * what[4] * what[6] if kind == "unit" else 150))
    for n, (_, tb, s) in enumerate(steps):
        share = min(1.0, (SUB * (tb + 1) - s) / SUB)
        for j in range(4):
            time_of.append(time_of[-1] + (900 + 900 * share) * (0.35 if j == 1 else 0.65 / 3))
    due = [(4 * (first_step[k] - LEAD), ring.index(("turn", k)) + 1) for k in range(2 * NT)]
    ring_at, r, done = [], 0, 0.0
    for quarter in range(4 * len(steps)):
        start = r
        r = max([r] + [entries for at, entries in due if at <= quarter])
        ahead = [(work[entries] - max(done, work[start])) / (time_of[at] - time_of[quarter])
                 for at, entries in due if at > quarter]
        done = max(done, work[r]) + max(ahead, default=0.0) * (time_of[quarter + 1] - time_of[quarter])
        while r < len(ring) and work[r + 1] <= done + 1e-3:
            r += 1
        ring_at.append(range(start, r))
    if len(ring) % 2:
        ring.append(("none", 0))
        ring_at[-1] = range(ring_at[-1].start, len(ring))
    assert ring_at[-1].stop == len(ring)
    return steps, first_step, chunks, ring, ring_at


def attention(nc, dram, T, C, H, F, shared):
    NT = T // TB
    NB = T // P
    SUB = TB // P
    D = C // H
    G = H // 4
    QK_ROWS = ALIBI + len(Q_PART) * D
    ROWS = QK_ROWS + 2
    steps, first_step, chunks, ring, ring_at = plan(NT, SUB)
    NSTEP, NTILE, NRING, NTB = len(steps), 4 * len(steps), len(ring), 2 * NT
    SLOTS = 3
    PSLOTS = 12
    LAG = 2
    assert NTILE % SLOTS == 0 and NTILE % PSLOTS == 0 and NRING % 2 == 0 and ROWS <= P

    with ExitStack() as ctx:
        def sb(name, shape, dt):
            return ctx.enter_context(nc.sbuf_tensor(name, shape, dt))

        def ps(name, shape, dt):
            return ctx.enter_context(nc.psum_tensor(name, shape, dt))

        def sem(name):
            return ctx.enter_context(nc.semaphore(name))

        Qs = sb("Qs", [P, NT, 4, TB], BF16)
        Vs = sb("Vs", [P, NB, 4, 2 * D], F32)
        probs = sb("probs", [P, PSLOTS, TB], F32)
        Ks, future, ident, seen_bits = shared.Ks, shared.future, shared.ident, shared.seen_bits
        chunk_max = sb("chunk_max", [P, NT, 4, SUB, chunks[-1]], F32)
        row_max = sb("row_max", [P, NT, 4, SUB], F32)
        neg_parts = sb("neg_parts", [P, NT, 2, 4, SUB], BF16)
        neg_rows = sb("neg_rows", [32, NT, P], BF16)
        acc = sb("acc", [P, 2, TB], F32)
        w_stage = sb("w_stage", [P, F], F32)

        max_psum = ps("max_psum", [P, 2, 2 * TB], F32)
        score_psum = ps("score_psum", [P, SLOTS, TB], F32)
        y_psum = ps("y_psum", [P, TB], F32)

        q_loaded = [sem(f"q_loaded_{c}") for c in range(NT)]
        k_loaded = [[sem(f"k_loaded_{p}_{c}") for c in range(NT)] for p in range(2)]
        v_loaded = [sem(f"v_loaded_{c}") for c in range(NT)]
        ring_ready = sem("ring_ready")
        ring_free = sem("ring_free")
        small_done = sem("small_done")
        neg_ready = sem("neg_ready")
        neg_rows_ready = sem("neg_rows_ready")
        max_loaded = [sem(f"max_loaded_{c}") for c in range(4)]
        scores_ready = sem("scores_ready")
        exp_done = sem("exp_done")
        pv_done = sem("pv_done")
        acc_copied = sem("acc_copied")
        y_stored = [sem("y_stored_0"), sem("y_stored_1")]
        seen_step = sem("seen_step")
        chunk_loaded = sem("chunk_loaded")
        chunk_stored = sem("chunk_stored")
        waits_passed = sem("waits_passed")
        block = ctx.enter_context(nc.Block())

        def load_q(sp, g, c):
            sp.dma_start(Qs[0:ALIBI, c], dram["alibi_q"].rearrange("(g j) r (n t) -> g n r j t", j=4, t=TB)[g, c]
                         ).then_inc(q_loaded[c], DMA)
            for n, part in enumerate(Q_PART):
                src = dram["parts"][part].rearrange("(a g j d) (n t) -> a g n d j t", a=2, j=4, d=D, t=TB)
                sp.dma_start(Qs[ALIBI + n * D:ALIBI + (n + 1) * D, c], src[0, g, c]).then_inc(q_loaded[c], DMA)

        def load_k(sp, g, p, c):
            for n, part in enumerate(K_PART):
                src = dram["parts"][part].rearrange("(a g j d) (n t) -> a g n d j t", a=2, j=4, d=D, t=TB)
                sp.dma_start(Ks[ALIBI + n * D:ALIBI + (n + 1) * D, p, c], src[1, g, c]).then_inc(k_loaded[p][c], DMA)

        def load_v(sp, g, c):
            sp.dma_start(Vs[:, SUB * c:SUB * (c + 1)].rearrange("p s j e -> p s (j e)"),
                         dram["v_ones"][g, :, SUB * c:SUB * (c + 1), :]).then_inc(v_loaded[c], DMA)

        Q_DMAS, K_DMAS = 1 + len(Q_PART), len(K_PART)
        CHUNKS = dram["ffn_w"].shape[0] // (G // 2)
        quiet = [k for k in range(NTB) if k % NT >= 2][:CHUNKS]
        assert len(quiet) == CHUNKS and CHUNKS * (G // 2) == dram["ffn_w"].shape[0]

        @block.sync
        def _(sp):
            for c in range(NT):
                load_q(sp, 0, c)
                load_k(sp, 0, 0, c)
                load_v(sp, 0, c)
            for c in range(NT):
                load_k(sp, 1, 1, c)

            def next_q(i, p, g):
                for c in range(NT):
                    sp.wait_ge(scores_ready, NTILE * i + 4 * first_step[NT * p + c + 1])
                    load_q(sp, g, c)

            def next_v(i, p, g):
                for c in range(NT):
                    n = first_step[NT * p + NT - 1] + SUB * (c + 1)
                    sp.wait_ge(pv_done, NSTEP * i + n + PSLOTS // 4)
                    load_v(sp, g, c)

            with sp.Fori(0, G // 2 - 1) as i:
                next_q(i, 0, 2 * i + 1)
                next_v(i, 0, 2 * i + 1)
                for c in range(NT):
                    load_k(sp, 2 * i + 2, 0, c)
                next_q(i, 1, 2 * i + 2)
                next_v(i, 1, 2 * i + 2)
                for c in range(NT):
                    load_k(sp, 2 * i + 3, 1, c)
            next_q(G // 2 - 1, 0, G - 1)
            next_v(G // 2 - 1, 0, G - 1)
            sp.dma_start(shared.w_proj[:], dram["w_proj"].rearrange("(k p) n -> p k n", p=P)).then_inc(shared.early_loaded, DMA)
            for rows, name in ((shared.b_proj, "b_proj"), (shared.s5, "s5")):
                sp.dma_start(rows[:], dram[name].rearrange("p (a c) -> p a c", a=2)).then_inc(shared.early_loaded, DMA)
            sp.dma_start(shared.ident_f[:], dram["ident_f"]).then_inc(shared.early_loaded, DMA)
            sp.dma_start(shared.scales[:], dram["scales"]).then_inc(shared.early_loaded, DMA)
            sp.wait_ge(chunk_stored, DMA * dram["ffn_w"].shape[0])
            w_early = shared.w_early
            sp.dma_start(w_early[:], dram["ffn_w_copy"][0:w_early.shape[1]].rearrange("n p f -> p n f")
                         ).then_inc(shared.early_loaded, DMA)
            sp.wait_ge(y_stored[0], DMA * (NT * (G // 2 - 1) + NT // 2 + 1) + 1)
            load_rows(sp, dram, shared, 0)

        @block.tensor
        def _(pe):
            pe.sem_inc(pv_done, PSLOTS // 4)
            pe.wait_ge(shared.const_loaded, CONST_DMAS * DMA)

            def ring_entry(i, r):
                kind, what = ring[r]
                pe.wait_ge(ring_free, NRING * i + r + 1)
                if kind == "turn":
                    pe.wait_ge(neg_ready, NTB * i + what + 1)
                    nc.tensor.transpose(max_psum[0:32, r % 2, 0:P // 2].bitcast(BF16),
                                        neg_parts[:, what % NT].rearrange("p c h u -> p (c h u)"), ident[:]
                                        ).then_inc(ring_ready, 1)
                    return
                if kind == "none":
                    nc.tensor.matmul(max_psum[:, r % 2, 0:P], ident[:], ident[:], start=True, stop=True
                                     ).then_inc(ring_ready, 1)
                    return
                p, tb, u, first, heads, c, blocks, _ = what
                if (u, first, c) == (0, 0, 0):
                    pe.wait_ge(q_loaded[tb], Q_DMAS * DMA * (2 * i + p + 1))
                    pe.wait_ge(k_loaded[p][tb], K_DMAS * DMA * (i + 1))
                for h in range(heads):
                    q_block = Qs[0:QK_ROWS, tb, first + h, u * P:(u + 1) * P]
                    for b in range(0, blocks, SUB):
                        w = min(SUB, blocks - b) * P
                        diag = 8 * c + b + w // P == SUB * tb + u + 1
                        at = h * (8 // heads) * P + b * P
                        mm = nc.tensor.matmul(max_psum[:, r % 2, at:at + w], q_block,
                                              Ks[0:QK_ROWS, p, (8 * c + b) // SUB, first + h, 0:w],
                                              start=True, stop=not diag)
                        if diag:
                            mm = nc.tensor.matmul(max_psum[:, r % 2, at + w - P:at + w], ident[:], future[:],
                                                  start=False, stop=True)
                mm.then_inc(ring_ready, 1)

            def score_tile(i, n, j):
                p, tb, s = steps[n]
                skip = max(0, s - SUB * tb) * P
                e = 4 * n + j
                out = score_psum[:, e % SLOTS, 0:TB - skip]
                diag = s >= SUB * tb
                pe.wait_ge(exp_done, NTILE * i + e + 1)
                mm = nc.tensor.matmul(out, Ks[0:ROWS, p, s // SUB, j, (s % SUB) * P:(s % SUB + 1) * P],
                                      Qs[0:ROWS, tb, j, skip:TB], start=True, stop=not diag)
                if diag:
                    mm = nc.tensor.matmul(out[:, 0:P], future[:], ident[:], start=False, stop=True)
                mm.then_inc(scores_ready, 1)

            def weigh(i, n):
                p, tb, s = steps[n]
                skip = max(0, s - SUB * tb) * P
                if s == 0:
                    pe.wait_ge(acc_copied, NTB * i + NT * p + tb + 1)
                if s == SUB * tb:
                    pe.wait_ge(v_loaded[tb], DMA * (2 * i + p + 1))
                pe.wait_ge(exp_done, NTILE * i + 4 * n + 4 + SLOTS)
                for j in range(4):
                    mm = nc.tensor.matmul(y_psum[32 * j:32 * j + 32, skip:TB], Vs[:, s, j, :],
                                          probs[:, (4 * n + j) % PSLOTS, 0:TB - skip],
                                          start=s == 0, stop=s == SUB * (tb + 1) - 1)
                mm.then_inc(pv_done, 1)

            with pe.Fori(0, G // 2) as i:
                for n in range(NSTEP):
                    p, tb, s = steps[n]
                    for j in range(4):
                        if s == 0 and j == 0:
                            if n == 0:
                                for r in ring_at[0]:
                                    ring_entry(i, r)
                            k = NT * p + tb
                            pe.wait_ge(max_loaded[k % 4], 2 * DMA * (NTB // 4 * i + k // 4 + 1))
                        score_tile(i, n, j)
                        if j == 1 and n >= LAG:
                            weigh(i, n - LAG)
                        if n or j:
                            for r in ring_at[4 * n + j]:
                                ring_entry(i, r)
                for n in range(NSTEP - LAG, NSTEP):
                    weigh(i, n)

        @block.scalar
        def _(act):
            act.sem_inc(exp_done, SLOTS)
            act.sem_inc(acc_copied, 1)
            for b in range(2):
                act.sem_inc(y_stored[b], 1)
            y_dst = dram["yT"].rearrange("g p (n t) -> g n p t", t=TB)

            def take_sums(i, k):
                act.wait_ge(pv_done, NSTEP * i + first_step[k + 1] + PSLOTS // 4)
                act.wait_ge(y_stored[k % 2], DMA * (NT * i + k // 2) + 1)
                nc.scalar.activation(acc[:, k % 2], y_psum[:], ACT.Copy).then_inc(acc_copied, 1)
                act.wait_ge(acc_copied, NTB * i + k + 2)
                act.dma_start(y_dst[2 * i + k // NT, k % NT], acc[:, k % 2]).then_inc(y_stored[k % 2], DMA)

            with act.Fori(0, G // 2) as i:
                for n in range(NSTEP):
                    p, tb, s = steps[n]
                    skip = max(0, s - SUB * tb) * P
                    act.wait_ge(pv_done, NSTEP * i + n + 1)
                    for j in range(4):
                        e = 4 * n + j
                        act.wait_ge(scores_ready, NTILE * i + e + 1)
                        nc.scalar.activation(probs[:, e % PSLOTS, 0:TB - skip], score_psum[:, e % SLOTS, 0:TB - skip],
                                             ACT.Exp).then_inc(exp_done, 1)
                        if s == LAG - 1 and n >= LAG and j == 2:
                            take_sums(i, NT * p + tb - 1)
                take_sums(i, NTB - 1)
            for b in range(2):
                act.wait_ge(y_stored[b], DMA * NT * (G // 2) + 1)

        @block.vector
        def _(dve):
            dve.sem_inc(ring_free, 2)

            def reduce_entry(i, r):
                kind, what = ring[r]
                dve.wait_ge(ring_ready, NRING * i + r + 1)
                if kind == "turn":
                    nc.vector.tensor_copy(neg_rows[:, what % NT], max_psum[0:32, r % 2, 0:P // 2].bitcast(BF16)
                                          ).then_inc(neg_rows_ready, 1)
                    dve.wait_ge(neg_rows_ready, NTB * i + what + 1)
                    dve.sem_inc(ring_free, 1)
                    return
                if kind == "none":
                    dve.sem_inc(ring_free, 1)
                    return
                p, tb, u, first, heads, c, blocks, last = what
                nc.vector.reduce_max(chunk_max[:, tb, first:first + heads, u, c],
                                     max_psum[:, r % 2].rearrange("p (h k) -> p h k", h=heads)[:, :, 0:blocks * P],
                                     AX_X).then_inc(ring_free, 1)
                if last:
                    small = 2 * (NTB * i + NT * p + tb)
                    dve.wait_ge(ring_free, NRING * i + r + 3)
                    nc.vector.reduce_max(row_max[:, tb], chunk_max[:, tb, :, :, 0:chunks[tb]], AX_X
                                         ).then_inc(small_done, 1)
                    dve.wait_ge(small_done, small + 1)
                    nc.vector.tensor_scalar_mul(neg_parts[:, tb, 0], row_max[:, tb], -1.0).then_inc(small_done, 1)
                    dve.wait_ge(small_done, small + 2)
                    nc.vector.scalar_tensor_tensor(out=neg_parts[:, tb, 1], in0=row_max[:, tb], scalar=-1.0,
                                                   in1=neg_parts[:, tb, 0], op0=ALU.mult, op1=ALU.subtract
                                                   ).then_inc(neg_ready, 1)

            def see_chunk(i, n):
                at = CHUNKS * i + n
                dve.wait_ge(chunk_loaded, DMA * at + DMA)
                dve.wait_ge(seen_step, at + 1)
                nc.vector.tensor_tensor(seen_bits[:], seen_bits[:], w_stage[:].bitcast(I32), ALU.bitwise_or
                                        ).then_inc(seen_step, 1)

            nc.vector.memset(seen_bits[:], 0).then_inc(seen_step, 1)
            with dve.Fori(0, G // 2) as i:
                for n in range(NSTEP):
                    p, tb, s = steps[n]
                    for j in range(4):
                        for r in ring_at[4 * n + j]:
                            reduce_entry(i, r)
                    if s == 6 and NT * p + tb in quiet:
                        see_chunk(i, quiet.index(NT * p + tb))
            low_step = shared.low_step
            dve.wait_ge(seen_step, dram["ffn_w"].shape[0] + 1)
            nc.vector.tensor_scalar(seen_bits[:], seen_bits[:], BEYOND_F32R, None, ALU.bitwise_and).then_inc(low_step, 1)
            dve.wait_ge(low_step, 1)
            nc.vector.reduce_max(shared.low_bits[:], seen_bits[:], AX_X).then_inc(low_step, 1)
            dve.wait_ge(low_step, 2)
            nc.vector.tensor_copy(shared.low_bits_f[:], shared.low_bits[:]).then_inc(low_step, 1)
            for k in range(C // P):
                normalise_y(dve, nc, shared, 0, k)

        @block.gpsimd
        def _(pool):
            def send_max(i, k):
                pool.wait_ge(neg_rows_ready, NTB * i + k + 1)
                pool.sem_inc(waits_passed, 1)
                for part in range(2):
                    pool.dma_start(Qs[QK_ROWS + part:QK_ROWS + part + 1, k % NT].rearrange("p j t -> p (j t)"),
                                   neg_rows[16 * part:16 * part + 16, k % NT]).then_inc(max_loaded[k % 4], DMA)

            def see_chunk(i, n):
                at = CHUNKS * i + n
                pool.dma_start(w_stage[:], dram["ffn_w"][at]).then_inc(chunk_loaded, DMA)
                pool.wait_ge(chunk_loaded, DMA * at + DMA)
                pool.sem_inc(waits_passed, 1)
                pool.dma_start(dram["ffn_w_copy"][at], w_stage[:]).then_inc(chunk_stored, DMA)
                pool.wait_ge(seen_step, at + 2)
                pool.wait_ge(chunk_stored, DMA * at + DMA)
                pool.sem_inc(waits_passed, 1)

            with pool.Fori(0, G // 2) as i:
                for k in range(NTB):
                    send_max(i, k)
                    if k in quiet:
                        see_chunk(i, quiet.index(k))


def load_rows(sp, dram, shared, t):
    src = dram["yT"].rearrange("g (j e) (n t) -> n g j e t", e=2 * HEAD, t=TB)
    rows = 4 * HEAD
    for g in range(src.shape[1]):
        at = rows * g % P
        for dst, e in ((shared.yT, 0), (shared.sums, HEAD)):
            sp.dma_start(dst[at:at + rows, rows * g // P], src[t, g, :, e:e + HEAD]).then_inc(shared.y_loaded, DMA)


def normalise_y(dve, nc, shared, t, k):
    yT, sums = shared.yT, shared.sums
    loads = 2 * DMA * (yT.shape[1] * P // (4 * HEAD))
    dve.wait_ge(shared.y_loaded, loads * t + loads)
    nc.vector.reciprocal(sums[:, k], sums[:, k]).then_inc(shared.inverted, 1)
    dve.wait_ge(shared.inverted, yT.shape[1] * t + k + 1)
    nc.vector.tensor_mul(yT[:, k], yT[:, k], sums[:, k]).then_inc(shared.y_ready, 1)


def ffn(nc, dram, T, C, H, F, shared):
    NT = T // TB
    SUB = TB // P
    BANKS = SUB // 2
    KC = C // P
    KF = F // P
    SPLITS = 3 * KF
    HT = 4 * KF
    EARLY_DMAS = 6
    RING = 4
    assert 2 * C == TB and KF > RING

    with ExitStack() as ctx:
        def sb(name, shape, dt):
            return ctx.enter_context(nc.sbuf_tensor(name, shape, dt))

        def ps(name, shape, dt):
            return ctx.enter_context(nc.psum_tensor(name, shape, dt))

        def sem(name):
            return ctx.enter_context(nc.semaphore(name))

        w_late = sb("w_late", [P, 2 * KF, F], F32)
        w_early, w_proj, b_proj, s5 = shared.w_early, shared.w_proj, shared.b_proj, shared.s5
        scales, ident = shared.scales, shared.ident_f
        yT, early_loaded = shared.yT, shared.early_loaded
        w1, w2 = w_early[:, 0:KC], w_early[:, KC:2 * KC]
        w5 = w_early[:, 2 * KC:3 * KC].rearrange("p a (b n) -> p (a b) n", n=C)
        w3, w4 = w_late[:, 0:KF], w_late[:, KF:2 * KF]
        minus_half = sb("minus_half", [P, SUB], F32)
        ones = sb("ones", [P, 1], F32)
        low_sum = sb("low_sum", [1, 1], I32)
        x = sb("x", [P, SUB, C], F32)
        z = sb("z", [P, SUB, C], F32)
        x1 = sb("x1", [P, SUB, C], F32)
        x1_kept = sb("x1_kept", [P, SUB, C], F32)
        out_sb = sb("out_sb", [P, SUB, C], F32)
        x1T_hi = sb("x1T_hi", [P, KC, TB], F32R)
        x1T_lo = sb("x1T_lo", [P, KC, TB], F32R)
        gate = sb("gate", [P, 2, TB], F32)
        full = sb("full_f", [P, RING, TB], F32)
        hid_hi = sb("hid_hi", [P, 2, KF, TB], F32R)
        hid_lo = sb("hid_lo", [P, 2, KF, TB], F32R)
        stats = sb("stats", [P, SUB, 6], F32)
        moments = sb("moments", [P, SUB, 2], F32)
        var_eps = sb("var_eps", [P, SUB], F32)
        rstd = sb("rstd", [P, SUB], F32)
        row_psum = ps("row_psum", [P, BANKS, 2, C], F32)
        turn_psum = ps("turn_psum", [P, KC, TB], F32)
        hid_psum = ps("hid_psum", [P, RING, TB], F32)

        w3_loaded = sem("w3_loaded")
        w4_loaded = sem("w4_loaded")
        ones_ready = sem("ones_ready_f")
        low_summed = sem("low_summed")
        branch_ready = sem("branch_ready")
        x_loaded = sem("x_loaded_f")
        proj_ready = sem("proj_ready")
        z_ready = sem("z_ready")
        stat_step = sem("stat_step")
        var_ready = sem("var_ready")
        rstd_ready = sem("rstd_ready")
        x1_ready = sem("x1_ready")
        kept_ready = sem("kept_ready")
        kept_used = sem("kept_used")
        turned = sem("turned")
        x1T_hi_ready = sem("x1T_hi_ready")
        x1T_ready = sem("x1T_ready")
        hid_ready = sem("hid_ready")
        gate_ready = sem("gate_ready")
        gated = sem("gated")
        hi_ready = sem("hi_ready")
        lo_ready = sem("lo_ready")
        down_ready = sem("down_ready")
        z2_ready = sem("z2_ready")
        sum_step = sem("sum_step")
        out_ready = sem("out_ready")
        out_stored = sem("out_stored")
        waits_passed = sem("waits_passed")
        block = ctx.enter_context(nc.Block())

        @block.sync
        def _(sp):
            sp.sem_inc(out_stored, 1)
            x_src = dram["x"].rearrange("(n s p) c -> n p s c", s=SUB, p=P)
            dst = dram["out"].rearrange("(n s p) c -> n p s c", s=SUB, p=P)

            def load(t, first):
                if not first:
                    sp.wait_ge(proj_ready, BANKS * t)
                    load_rows(sp, dram, shared, t)
                    sp.wait_ge(z_ready, BANKS * t + 1)
                sp.dma_start(x[:], x_src[t]).then_inc(x_loaded, DMA)

            def store(t):
                sp.wait_ge(out_ready, SUB * t + SUB)
                sp.dma_start(dst[t], out_sb[:]).then_inc(out_stored, DMA)

            load(0, True)
            for lay, loaded in enumerate((w3_loaded, w4_loaded)):
                for k in range(KF):
                    sp.dma_start(w_late[:, KF * lay + k], dram["ffn_w_copy"][3 * KC + KF * lay + k]
                                 ).then_inc(loaded, DMA)
            load(1, False)
            with sp.Fori(1, NT - 1) as i:
                load(i + 1, False)
                store(i - 1)
            store(NT - 2)
            store(NT - 1)
            sp.wait_ge(out_stored, DMA * NT + 1)

        @block.gpsimd
        def _(pool):
            nc.gpsimd.memset(minus_half[:], -0.5).then_inc(rstd_ready, 1)
            pool.wait_ge(rstd_ready, 1)

            def power(n):
                pool.wait_ge(var_ready, n + 1)
                nc.gpsimd.tensor_tensor(rstd[:], var_eps[:], minus_half[:], ALU.pow).then_inc(rstd_ready, 1)

            def keep(i):
                pool.wait_ge(x1_ready, SUB * i + SUB)
                pool.wait_ge(kept_used, i + 1)
                pool.sem_inc(waits_passed, 1)
                nc.gpsimd.tensor_copy(x1_kept[:], x1[:]).then_inc(kept_ready, 1)

            power(0)
            keep(0)
            power(1)
            with pool.Fori(1, NT - 1) as i:
                power(2 * i)
                keep(i)
                power(2 * i + 1)
            power(2 * NT - 2)
            keep(NT - 1)
            power(2 * NT - 1)

        @block.tensor
        def _(pe):
            def project_out(t, first):
                pe.wait_ge(shared.y_ready, KC * t + KC)
                if not first:
                    pe.wait_ge(z2_ready, BANKS * t - BANKS + 1)
                for s in range(SUB):
                    for k in range(KC):
                        mm = nc.tensor.matmul(row_psum[:, s // 2, s % 2], yT[:, k, s * P:(s + 1) * P], w_proj[:, k],
                                              start=k == 0, stop=k == KC - 1)
                    if s % 2:
                        mm.then_inc(proj_ready, 1)

            def transpose(t):
                for s in range(SUB):
                    pe.wait_ge(x1_ready, SUB * t + s + 1)
                    for k in range(KC):
                        mm = nc.tensor.transpose(turn_psum[:, k, s * P:(s + 1) * P], x1[:, s, k * P:(k + 1) * P], ident[:])
                mm.then_inc(turned, 1)

            def layers(i, last, exact):
                def weights(ap):
                    return ap.bitcast(F32R) if exact else ap

                def parts(hi, lo):
                    return enumerate((hi, lo) if exact else (hi.bitcast(F32), lo.bitcast(F32)))

                pe.wait_ge(x1T_ready, KC * i + KC)
                for m in range(KF):
                    if m >= 2:
                        pe.wait_ge(gated, KF * i + m + 1)
                    for t, w in enumerate((w1, w2)):
                        for k in range(KC):
                            for c, part in parts(x1T_hi[:, k], x1T_lo[:, k]):
                                mm = nc.tensor.matmul(hid_psum[:, (2 * m + t) % RING], weights(w[:, k, m * P:(m + 1) * P]),
                                                      part, start=(k, c) == (0, 0), stop=(k, c) == (KC - 1, 1))
                        mm.then_inc(hid_ready, 1)
                for lay, (w, loaded) in enumerate(((w3, w3_loaded), (w4, w4_loaded))):
                    pe.wait_ge(loaded, DMA * KF)
                    for m in range(KF):
                        before = SPLITS * i + KF * lay + m
                        if lay == 0 and m == 0:
                            pe.wait_ge(gated, KF * i + KF + 1)
                        elif lay == 1 or m >= RING:
                            pe.wait_ge(hi_ready, before + KF - RING + 1)
                        for k in range(KF):
                            if m == 0:
                                pe.wait_ge(lo_ready, before + k + 1 + RING)
                            for c, part in parts(hid_hi[:, lay, k], hid_lo[:, lay, k]):
                                mm = nc.tensor.matmul(hid_psum[:, m % RING], weights(w[:, k, m * P:(m + 1) * P]),
                                                      part, start=(k, c) == (0, 0), stop=(k, c) == (KF - 1, 1))
                        mm.then_inc(hid_ready, 1)
                        if not last and (lay, m) == PROJECT_AFTER:
                            project_out(i + 1, False)
                        if not last and (lay, m) == TRANSPOSE_AFTER:
                            transpose(i + 1)
                if not last:
                    pe.wait_ge(z_ready, BANKS * i + 2 * BANKS + 1)
                else:
                    pe.wait_ge(z2_ready, BANKS * i + 1)
                for s in range(SUB):
                    for k in range(KF):
                        if s == 0:
                            pe.wait_ge(lo_ready, SPLITS * i + 2 * KF + k + 1 + RING)
                        for c, part in parts(hid_hi[:, 0, k, s * P:(s + 1) * P], hid_lo[:, 0, k, s * P:(s + 1) * P]):
                            mm = nc.tensor.matmul(row_psum[:, s // 2, s % 2], part, weights(w5[:, k]),
                                                  start=(k, c) == (0, 0), stop=(k, c) == (KF - 1, 1))
                    if s % 2:
                        mm.then_inc(down_ready, 1)

            pe.wait_ge(early_loaded, EARLY_DMAS * DMA)
            project_out(0, True)
            pe.wait_ge(shared.low_step, 3)
            pe.wait_ge(ones_ready, 1)
            nc.tensor.matmul(turn_psum[0:1, 0, 0:1], shared.low_bits_f[:], ones[:], start=True, stop=True).then_inc(low_summed, 1)
            pe.wait_ge(branch_ready, 1)
            transpose(0)
            beyond = pe.value_load(low_sum[0:1, 0:1])
            with pe.If(beyond == 0):
                with pe.Fori(0, NT - 1) as i:
                    layers(i, False, True)
                layers(NT - 1, True, True)
            with pe.Else():
                with pe.Fori(0, NT - 1) as i:
                    layers(i, False, False)
                layers(NT - 1, True, False)

        @block.scalar
        def _(act):
            act.wait_ge(early_loaded, EARLY_DMAS * DMA)

            def split_x1T(t):
                act.wait_ge(turned, t + 1)
                for k in range(KC):
                    nc.scalar.activation(x1T_hi[:, k], turn_psum[:, k], ACT.Copy).then_inc(x1T_hi_ready, 1)

            def layers(i, last):
                def gate_hi(m):
                    act.wait_ge(gated, KF * i + m + 3)
                    nc.scalar.activation(hid_hi[:, 0, m], full[:, m % RING], ACT.Copy).then_inc(hi_ready, 1)

                for m in range(KF):
                    act.wait_ge(hid_ready, HT * i + 2 * m + 1)
                    act.wait_ge(gated, KF * i + m + 1)
                    nc.scalar.activation(gate[:, m % 2], hid_psum[:, (2 * m) % RING], ACT.Silu,
                                         scale=scales[:, 0, m:m + 1]).then_inc(gate_ready, 1)
                    if m >= 1:
                        gate_hi(m - 1)
                gate_hi(KF - 1)
                for lay in range(2):
                    for m in range(KF):
                        n = KF * (1 + lay) + m
                        act.wait_ge(hid_ready, HT * i + KF + n + 1)
                        act.wait_ge(lo_ready, SPLITS * i + n + 1)
                        nc.scalar.activation(full[:, m % RING], hid_psum[:, m % RING], ACT.Gelu,
                                             scale=scales[:, 2 + lay, m:m + 1])
                        nc.scalar.activation(hid_hi[:, 1 - lay, m], hid_psum[:, m % RING], ACT.Gelu,
                                             scale=scales[:, 2 + lay, m:m + 1]).then_inc(hi_ready, 1)
                        if not last and (lay, m) == TRANSPOSE_AFTER:
                            split_x1T(i + 1)

            split_x1T(0)
            with act.Fori(0, NT - 1) as i:
                layers(i, False)
            layers(NT - 1, True)

        @block.vector
        def _(dve):
            dve.sem_inc(z_ready, 1)
            dve.sem_inc(z2_ready, 1)
            dve.sem_inc(kept_used, 1)
            dve.sem_inc(gated, 2)
            dve.sem_inc(lo_ready, RING)

            nc.vector.memset(ones[:], 1.0).then_inc(ones_ready, 1)
            dve.wait_ge(low_summed, 1)
            nc.vector.tensor_copy(low_sum[:], turn_psum[0:1, 0, 0:1]).then_inc(branch_ready, 1)
            dve.wait_ge(early_loaded, EARLY_DMAS * DMA)

            def moments_of(n, src):
                for s in range(SUB):
                    nc.vector.bn_stats(stats[:, s], src[:, s]).then_inc(stat_step, 1)
                dve.wait_ge(stat_step, 2 * SUB * n + SUB)
                dve.sem_inc(waits_passed, 1)
                for s in range(SUB):
                    nc.vector.bn_aggr(moments[:, s], stats[:, s]).then_inc(stat_step, 1)
                dve.wait_ge(stat_step, 2 * SUB * n + 2 * SUB)
                nc.vector.tensor_scalar_add(var_eps[:], moments[:, :, 1], EPS).then_inc(var_ready, 1)

            def normalise(n, src, dst, ready):
                dve.wait_ge(rstd_ready, n + 2)
                for s in range(SUB):
                    nc.vector.tensor_scalar(dst[:, s], src[:, s], moments[:, s, 0:1], rstd[:, s:s + 1],
                                            ALU.subtract, ALU.mult).then_inc(ready, 1)

            def first_sum(t, n):
                dve.wait_ge(x_loaded, DMA * t + DMA)
                for b in range(BANKS):
                    add = nc.vector.tensor_add(z[:, 2 * b:2 * b + 2], x[:, 2 * b:2 * b + 2], b_proj[:])
                add.then_inc(sum_step, 1)
                dve.wait_ge(sum_step, t + 1)
                for b in range(BANKS):
                    dve.wait_ge(proj_ready, BANKS * t + b + 1)
                    nc.vector.tensor_add(z[:, 2 * b:2 * b + 2], z[:, 2 * b:2 * b + 2], row_psum[:, b]).then_inc(z_ready, 1)
                dve.wait_ge(z_ready, BANKS * t + BANKS + 1)
                moments_of(n, z)

            def second_sum(t, n):
                for b in range(BANKS):
                    dve.wait_ge(down_ready, BANKS * t + b + 1)
                    nc.vector.tensor_mul(z[:, 2 * b:2 * b + 2], row_psum[:, b], s5[:]).then_inc(z2_ready, 1)
                dve.wait_ge(z2_ready, BANKS * t + BANKS + 1)
                dve.wait_ge(kept_ready, t + 1)
                nc.vector.tensor_add(z[:], z[:], x1_kept[:]).then_inc(kept_used, 1)
                dve.wait_ge(kept_used, t + 2)
                moments_of(n, z)

            def normalise_out(t, n):
                dve.wait_ge(out_stored, DMA * t + 1)
                normalise(n, z, out_sb, out_ready)

            def split_x1T(t):
                for k in range(KC):
                    dve.wait_ge(x1T_hi_ready, KC * t + k + 1)
                    nc.vector.tensor_sub(x1T_lo[:, k], turn_psum[:, k], x1T_hi[:, k].bitcast(F32)).then_inc(x1T_ready, 1)

            def layers(i, first, last):
                def split(n):
                    lay, m = n // KF, n % KF
                    dve.wait_ge(hi_ready, SPLITS * i + n + 1)
                    nc.vector.tensor_sub(hid_lo[:, lay % 2, m], full[:, m % RING], hid_hi[:, lay % 2, m].bitcast(F32)
                                         ).then_inc(lo_ready, 1)

                for m in range(KF):
                    dve.wait_ge(gate_ready, KF * i + m + 1)
                    dve.wait_ge(hid_ready, HT * i + 2 * m + 2)
                    dve.wait_ge(lo_ready, SPLITS * i + m + 1)
                    nc.vector.scalar_tensor_tensor(out=full[:, m % RING], in0=hid_psum[:, (2 * m + 1) % RING],
                                                   scalar=scales[:, 1, m:m + 1], in1=gate[:, m % 2],
                                                   op0=ALU.mult, op1=ALU.mult).then_inc(gated, 1)
                    if m >= 1:
                        split(m - 1)
                split(KF - 1)
                if not first:
                    dve.wait_ge(x1_ready, SUB * i + SUB)
                    second_sum(i - 1, 2 * i)
                split(KF)
                split(KF + 1)
                if not first:
                    normalise_out(i - 1, 2 * i)
                for m in range(2, KF):
                    split(KF + m)
                    if not last and m - 2 < KC:
                        normalise_y(dve, nc, shared, i + 1, m - 2)
                    if not last and (0, m) == PROJECT_AFTER:
                        if not first:
                            dve.wait_ge(out_ready, SUB * i)
                        first_sum(i + 1, 2 * i + 1)
                    if not last and (0, m - 1) == PROJECT_AFTER:
                        dve.wait_ge(kept_ready, i + 1)
                        normalise(2 * i + 1, z, x1, x1_ready)
                for m in range(KF):
                    split(2 * KF + m)
                    if not last and (1, m) == TRANSPOSE_AFTER:
                        split_x1T(i + 1)

            first_sum(0, 0)
            normalise(0, z, x1, x1_ready)
            split_x1T(0)
            layers(0, True, False)
            with dve.Fori(1, NT - 1) as i:
                layers(i, False, False)
            layers(NT - 1, False, True)
            dve.wait_ge(x1_ready, SUB * NT)
            second_sum(NT - 1, 2 * NT - 1)
            normalise_out(NT - 1, 2 * NT - 1)


class Shared:
    pass


def build(nc, dram, T, C, H, F):
    KC, KF, NT = C // P, F // P, T // TB
    with ExitStack() as ctx:
        def sb(name, shape, dt):
            return ctx.enter_context(nc.sbuf_tensor(name, shape, dt))

        def sem(name):
            return ctx.enter_context(nc.semaphore(name))

        shared = Shared()
        shared.const_loaded = sem("const_loaded")
        shared.w_early = sb("w_early", [P, 3 * KC, F], F32)
        shared.w_proj = sb("w_proj", [P, KC, C], F32)
        shared.b_proj = sb("b_proj", [P, 2, C], F32)
        shared.s5 = sb("s5", [P, 2, C], F32)
        shared.scales = sb("scales", [P, 4, KF], F32)
        shared.ident_f = sb("ident_f", [P, P], F32)
        shared.early_loaded = sem("early_loaded")
        shared.yT = sb("yT", [P, KC, TB], F32)
        shared.sums = sb("sums", [P, KC, TB], F32)
        shared.y_loaded = sem("y_loaded")
        shared.inverted = sem("inverted")
        shared.y_ready = sem("y_ready")
        shared.low_bits = sb("low_bits", [P, 1], I32)
        shared.low_bits_f = sb("low_bits_f", [P, 1], F32)
        shared.low_step = sem("low_step")
        with nc.sbuf_tensor("Ks", [P, 2, NT, 4, TB], BF16) as Ks, nc.sbuf_tensor("future", [P, P], BF16) as future, \
                nc.sbuf_tensor("ident", [P, P], BF16) as ident, nc.sbuf_tensor("seen_bits", [P, F], I32) as seen_bits:
            shared.Ks = Ks
            shared.future = future
            shared.ident = ident
            shared.seen_bits = seen_bits
            project(nc, dram, T, C, H, shared)
            attention(nc, dram, T, C, H, F, shared)
        ffn(nc, dram, T, C, H, F, shared)


def kernel(**inputs):
    import numpy as np
    import concourse.bacc as bacc
    from concourse import mybir as _mybir
    from concourse.bass_utils import run_bass_kernel_spmd

    x = np.ascontiguousarray(inputs["L0_attn_x"])[0]
    T, C = x.shape
    H = 16
    F = inputs["L0_ffn_w1_w"].shape[0]
    w_attn = np.ascontiguousarray(inputs["L0_attn_W_attn"])
    b_attn = np.ascontiguousarray(inputs["L0_attn_b_attn"])

    def bf16_bits(a):
        return (np.ascontiguousarray(a, dtype=np.float32).view(np.uint32) >> 16).astype(np.uint16)

    def rows(v):
        return np.ascontiguousarray(np.broadcast_to(v, (128, v.shape[0])))

    def columns(v):
        return np.ascontiguousarray(np.asarray(v).reshape(-1, 128).T)

    def chunks(w):
        blocks = np.asarray(w).T.reshape(-1, 128, w.shape[0]).transpose(1, 0, 2)
        return blocks.reshape(128, -1, F).transpose(1, 0, 2)

    pos = np.arange(T)
    slope = 0.5 ** np.arange(1, H + 1)[:, None]
    alibi_k = np.stack([pos % 128, pos - pos % 128, np.ones(T), np.ones(T)])
    alibi_q = np.stack([slope + 0 * pos, slope + 0 * pos, -slope * (pos % 128), -slope * (pos - pos % 128)], axis=1)
    future = np.where(np.arange(128)[None, :] > np.arange(128)[:, None], -1e30, 0.0)
    arrays = {
        "x": x,
        "xT": np.ascontiguousarray(x.T),
        "w_attn": w_attn,
        "b_qk": columns(b_attn[:2 * C]),
        "b_v": rows(b_attn[2 * C:]),
        "w_proj": np.ascontiguousarray(inputs["L0_attn_W_proj"]),
        "b_proj": rows(np.tile(np.asarray(inputs["L0_attn_b_proj"]), 2)),
        "ffn_w": np.concatenate([chunks(inputs[f"L0_ffn_{n}_w"]) for n in ("w1", "w2", "w3", "h1", "h2")]),
        "scales": np.ascontiguousarray(np.stack([columns(inputs[f"L0_ffn_{n}_s"]) for n in ("w1", "w2", "h1", "h2")], 1)),
        "s5": rows(np.tile(np.asarray(inputs["L0_ffn_w3_s"]), 2)),
        "ident_f": np.eye(128, dtype=np.float32),
        "ident": bf16_bits(np.eye(128)),
        "future": bf16_bits(future),
        "alibi_k": bf16_bits(alibi_k),
        "alibi_q": bf16_bits(alibi_q),
    }
    nc = bacc.Bacc("TRN2", target_bir_lowering=False, num_devices=1)
    dram = {}
    for name, a in arrays.items():
        ap = nc.dram_tensor(name + "_dram", a.shape, _mybir.dt.from_np(a.dtype), kind="ExternalInput").ap()
        dram[name] = ap.bitcast(_mybir.dt.bfloat16) if a.dtype == np.uint16 else ap
    dram["parts"] = nc.dram_tensor("parts_dram", (3, 2 * C, T), _mybir.dt.bfloat16, kind="Internal").ap()
    dram["v_ones"] = nc.dram_tensor("v_ones_dram", (H // 4, 128, T // 128, 128), _mybir.dt.float32, kind="Internal").ap()
    dram["yT"] = nc.dram_tensor("yT_dram", (H // 4, 128, T), _mybir.dt.float32, kind="Internal").ap()
    dram["ffn_w_copy"] = nc.dram_tensor("ffn_w_copy_dram", arrays["ffn_w"].shape, _mybir.dt.float32, kind="Internal").ap()
    dram["out"] = nc.dram_tensor("out_dram", (T, C), _mybir.dt.float32, kind="ExternalOutput").ap()
    build(nc, dram, T, C, H, F)
    r = run_bass_kernel_spmd(nc, [{k + "_dram": v for k, v in arrays.items()}], core_ids=[0])
    return r.results[0]["out_dram"].reshape(1, T, C)
```
